# Optimizing a Trainium2 kernel written in Bass

```python
import numpy as np
import jax
import jax.numpy as jnp

def _softmax(x, axis=-1):
    return jax.nn.softmax(x, axis=axis)

def _gelu(x):
    return jax.nn.gelu(x, approximate=True)

def _silu(x):
    return jax.nn.silu(x)

def _sigmoid(x):
    return jax.nn.sigmoid(x)

def _layernorm(x, axis=-1, eps=1e-05):
    m = jnp.mean(x, axis=axis, keepdims=True)
    v = jnp.var(x, axis=axis, keepdims=True)
    return (x - m) / jnp.sqrt(v + eps)

def _scatter_add(tgt, idx, src, axis=0):
    return tgt.at[idx].add(src)

def _segment_sum(src, seg, n):
    return jax.ops.segment_sum(src, seg, n)
kernel_name = 'mk_adj_preln_d2_adj_r2_87eb56'

def setup_inputs(seed: int=0):
    np.random.seed(seed)
    _w = jnp.asarray

    def _rec_inputs():
        import jax
        import jax.numpy as jnp
        _gk = jax.random.key(seed)
        x = -9.806e-05 + 1 * jax.random.normal(jax.random.fold_in(_gk, 1), (4096, 64), jnp.float32)
        _a = jax.random.bernoulli(jax.random.fold_in(_gk, 2), 0.000488281, (4096, 4096))
        adj = _a.astype(jnp.int32)
        return (x, adj)
    x, adj = _rec_inputs()

    def _L0_gnn_setup():
        import jax, jax.numpy as jnp
        import numpy as np
        ALPHA = 0.2
        NEG_BIG = -9000000000000000.0
        key = jax.random.key(seed)
        k1, k2, k3, k4, k5 = jax.random.split(key, 5)
        N, M, F_in, F_out = (4096, 4096, 64, 64)
        item_embs = jax.random.normal(k1, (N, F_in), dtype=jnp.float32)
        entity_embs = jax.random.normal(k2, (M, F_in), dtype=jnp.float32)
        adj = jax.random.randint(k3, (N, M), 0, 2, dtype=jnp.int32)
        W = jax.random.normal(k4, (F_in, F_out), dtype=jnp.float32)
        a = jax.random.normal(k5, (2 * F_out, 1), dtype=jnp.float32)
        return {'item_embs': item_embs, 'entity_embs': entity_embs, 'adj': adj, 'W': W, 'a': a}
    _L0_gnn_all = _L0_gnn_setup()
    _L0_gnn_in = {k: v for k, v in _L0_gnn_all.items() if k in ('entity_embs', 'W', 'a')}
    del _L0_gnn_all

    def _L1_gnn_setup():
        import jax, jax.numpy as jnp
        import numpy as np
        ALPHA = 0.2
        NEG_INF = -9000000000000000.0
        key = jax.random.key(seed)
        k1, k2, k3, k4 = jax.random.split(key, 4)
        N, F_IN, F_OUT = (512, 64, 64)
        h = jax.random.normal(k1, (N, F_IN), dtype=jnp.float32)
        adj = jax.random.randint(k2, (N, N), 0, 2, dtype=jnp.int32)
        lim_W = 1.414 * np.sqrt(6.0 / (F_IN + F_OUT))
        W = jax.random.uniform(k3, (F_IN, F_OUT), minval=-lim_W, maxval=lim_W, dtype=jnp.float32)
        lim_a = 1.414 * np.sqrt(6.0 / (2 * F_OUT + 1))
        a = jax.random.uniform(k4, (2 * F_OUT, 1), minval=-lim_a, maxval=lim_a, dtype=jnp.float32)
        return {'h': h, 'adj': adj, 'W': W, 'a': a}
    _L1_gnn_all = _L1_gnn_setup()
    _L1_gnn_in = {k: v for k, v in _L1_gnn_all.items() if k in ('W', 'a')}
    del _L1_gnn_all
    return {'x': x, 'adj': adj, 'L0_gnn_entity_embs': _L0_gnn_in['entity_embs'], 'L0_gnn_W': _L0_gnn_in['W'], 'L0_gnn_a': _L0_gnn_in['a'], 'L1_gnn_W': _L1_gnn_in['W'], 'L1_gnn_a': _L1_gnn_in['a']}

def reference(x, adj, L0_gnn_entity_embs, L0_gnn_W, L0_gnn_a, L1_gnn_W, L1_gnn_a):
    import jax
    import jax.numpy as jnp

    def _L0_gnn_ref(item_embs, entity_embs, adj, W, a):
        import jax, jax.numpy as jnp
        import numpy as np
        ALPHA = 0.2
        NEG_BIG = -9000000000000000.0
        F_out = W.shape[1]
        Wh = item_embs @ W
        We = entity_embs @ W
        a1 = a[:F_out, 0]
        a2 = a[F_out:, 0]
        scores = (Wh @ a1)[:, None] + (We @ a2)[None, :]
        e = jnp.where(scores > 0, scores, ALPHA * scores)
        e = jnp.where(adj > 0, e, NEG_BIG)
        attention = jax.nn.softmax(e, axis=1)
        entity_emb_weighted = attention @ entity_embs
        h_prime = entity_emb_weighted + item_embs
        return jax.nn.elu(h_prime)

    def _L1_gnn_ref(h, adj, W, a):
        import jax, jax.numpy as jnp
        import numpy as np
        ALPHA = 0.2
        NEG_INF = -9000000000000000.0
        F_OUT = W.shape[1]
        Wh = h @ W
        a1, a2 = (a[:F_OUT, 0], a[F_OUT:, 0])
        e = (Wh @ a1)[:, None] + (Wh @ a2)[None, :]
        e = jax.nn.leaky_relu(e, negative_slope=ALPHA)
        scores = jnp.where(adj > 0, e, jnp.float32(NEG_INF))
        attention = jax.nn.softmax(scores, axis=1)
        h_prime = attention @ Wh
        return jax.nn.elu(h_prime)
    h = jnp.maximum(_layernorm(x, axis=-1), 0.0)
    x = x + _L0_gnn_ref(h, L0_gnn_entity_embs, adj, L0_gnn_W, L0_gnn_a)
    h = jnp.maximum(_layernorm(x, axis=-1), 0.0)
    x = x + _L1_gnn_ref(h, adj, L1_gnn_W, L1_gnn_a)
    return x

_drawn_inputs = setup_inputs


def setup_inputs(seed=0):
    import zlib

    import numpy as np

    out = dict(_drawn_inputs(seed))
    spreads = {}
    factors = {}
    for name, (base, spread) in spreads.items():
        noise = np.random.default_rng([zlib.crc32(name.encode()), seed]).standard_normal(out[name].shape)
        drawn = base * np.exp(spread * noise) if base else spread * noise
        out[name] = jnp.asarray(drawn.astype(out[name].dtype))
    for name, factor in factors.items():
        out[name] = (out[name] * factor).astype(out[name].dtype)
    return out
```

```python
import concourse.bass as bass
from concourse import mybir
from contextlib import ExitStack


N = 4096
F = 64
P = 128
TILES = N // P
GT = 4
GROUPS = TILES // GT
ROWS = 13
CODES = -(-P // ROWS)
POS = CODES * P
POSBITS = 11
VALID = float(1 << POSBITS)
SEG = 64
NSEG = POS // SEG
TOP = 24
CH = 3
ENTRIES = CH * P
NCH = CH * GT
VF = F + 2
MROWS = CODES * ROWS
BIG = 1.0e30
FLOOR = -1.0e20
SLOPE = 0.2
EPS = 1e-5
NEWTON = 3


def const_columns():
    at, where = 0, {}
    for name, width in (("ident", P), ("code", CODES), ("before", P), ("tile", GT), ("block", 1),
                        ("slot", ENTRIES), ("entry", CH), ("top", TOP), ("group", CODES), ("bit", ROWS)):
        where[name] = (at, at + width)
        at += width
    return where, at


def graph_attention(nc, x, adj, ent, W0, a0, W1, a1, consts, places, tab0, tab1, out):
    fp32 = mybir.dt.float32
    bf16 = mybir.dt.bfloat16
    i32 = mybir.dt.int32
    ALU = mybir.AluOpType
    ACT = mybir.ActivationFunctionType
    X = mybir.AxisListType.X
    where, width = const_columns()

    x_v = x.rearrange("(t p) f -> p t f", p=P)
    out_v = out.rearrange("(t p) f -> p t f", p=P)
    ent_v = ent.rearrange("(t p) f -> p t f", p=P)
    tab_v = [t.rearrange("(t p) f -> p t f", p=P) for t in (tab0, tab1)]
    tab = [tab0, tab1]

    ctx = ExitStack()
    with ctx:
        def sb(name, shape, dt=fp32):
            return ctx.enter_context(nc.sbuf_tensor(name, shape, dt))

        def ps(name, shape):
            return ctx.enter_context(nc.psum_tensor(name, shape, fp32))

        def sem(name):
            return ctx.enter_context(nc.semaphore(name))

        cst = sb("cst", [P, width])
        ident = cst[:, where["ident"][0]:where["ident"][1]]
        tile_of = cst[:, where["tile"][0]:where["tile"][1]]
        slot_no = cst[:, where["slot"][0]:where["slot"][1]]
        entry_no = cst[:, where["entry"][0]:where["entry"][1]]
        top_no = cst[:, where["top"][0]:where["top"][1]]
        group_no = cst[:, where["group"][0]:where["group"][1]]
        code_w = sb("code_w", [P, CODES], bf16)
        before = sb("before", [P, P], bf16)
        bit_w = sb("bit_w", [P, ROWS], i32)
        place_w = sb("place_w", [2, POS], bf16)
        ones2 = sb("ones2", [2, P], bf16)
        ones = sb("ones", [P, P])
        W0s = sb("W0s", [F, F])
        W0T = sb("W0T", [F, F])
        a0s = sb("a0s", [F, 2])
        a0b = sb("a0b", [F, 2, P])
        W1e = sb("W1e", [F, VF])
        W1T = sb("W1T", [F, F])
        a1s = sb("a1s", [F, 2])
        wbc = sb("wbc", [P, 2, F])
        xs = sb("xs", [P, TILES, F])
        h0 = sb("h0", [P, TILES, F])
        x1 = xs
        V = [sb("V0", [P, TILES, VF]), sb("V1", [P, TILES, VF])]
        s = [sb("s0", [P, TILES]), sb("s1", [P, TILES])]
        sumV = [sb("sumV0", [P, F + 1]), sb("sumV1", [P, F + 1])]
        A = sb("A", [P, GT, N], i32)
        edges = sb("edges", [P, 2, N], bf16)
        codes = sb("codes", [P, CODES, GT, TILES])
        keys = sb("keys", [P, POS])
        place_f = keys[0:2, :]
        slots = sb("slots", [P, NSEG, 8])
        top = sb("top", [P, TOP])
        over = sb("over", [P, 4])
        kept = sb("kept", [P, TOP + 2])
        isv = sb("isv", [P, TOP])
        cnt = sb("cnt", [P, 1])
        cntb = sb("cntb", [P, 1], bf16)
        end = sb("end", [P, 1])
        R = sb("R", [P, ENTRIES])
        Xbd = sb("Xbd", [P, GT, TOP + 2])
        dist = sb("dist", [P, NCH])
        hit = sb("hit", [P, NCH, TOP])
        keyi = sb("keyi", [P, NCH], i32)
        grp = sb("grp", [P, NCH], i32)
        col = sb("col", [P, NCH], i32)
        code = sb("code", [P, NCH], i32)
        biti = sb("biti", [P, NCH, ROWS], i32)
        bitb = sb("bitb", [P, NCH, ROWS], bf16)
        grpb = sb("grpb", [P, NCH, CODES], bf16)
        mask = sb("mask", [P, NCH, MROWS], bf16)
        R0 = mask[:, :, :].rearrange("p n m -> p (n m)").bitcast(fp32)[:, 0:ENTRIES]
        pen = sb("pen", [P, GROUPS, NCH, MROWS], bf16)
        idx_all = sb("idx_all", [P, GROUPS * NCH], i32)
        idx = [sb("idxa", [P, NCH], i32), sb("idxb", [P, NCH], i32)]
        flag = sb("flag", [1, 1], i32)
        Vg = [sb("Vga", [P, NCH, VF]), sb("Vgb", [P, NCH, VF])]
        wT = sb("wT", [P, NCH, P])
        E1 = sb("E1", [P, GT, ENTRIES])
        E2 = sb("E2", [P, GT, ENTRIES])
        PT = sb("PT", [P, NCH, P])
        Mx = sb("Mx", [P, GT])
        Mc = sb("Mc", [P, GT])
        sM = sb("sM", [P, GT])
        guard = sb("guard", [P, GT])
        bias1 = sb("bias1", [P, GT])
        bias2 = sb("bias2", [P, GT])
        empty = sb("empty", [P, GT])
        att = sb("att", [P, GT, F + 1])
        rden = sb("rden", [P, GT])
        hp = sb("hp", [P, GT, F])
        neg = sb("neg", [P, GT, F])
        en = sb("en", [P, GT, F])
        y = sb("y", [P, GT, F])
        outs = [sb("outa", [P, GT, F]), sb("outb", [P, GT, F])]
        sT = dist[:, 0:1]
        h1 = sb("h1", [P, GT, F])
        h1T = sb("h1T", [F, GT, P])
        ln = {n: sb("ln_" + n, [P, GT]) for n in ("sum", "nmean", "ssq", "var", "rstd")}
        lnc, lnq = hp, y
        ln0 = {n: sb("ln0_" + n, [P, TILES]) for n in ("sum", "nmean", "ssq", "var", "rstd")}
        big = pen[:, :, :, :].rearrange("p a b c -> p (a b c)").bitcast(fp32)
        lnc0 = big[:, 0:TILES * F].rearrange("p (t f) -> p t f", f=F)
        lnq0 = big[:, TILES * F:2 * TILES * F].rearrange("p (t f) -> p t f", f=F)

        low = ps("low", [P, 3, 512])
        sums = ps("sums", [P, 512])
        work = ps("work", [P, 3, 512])
        kbank = ps("kbank", [P, 512])
        offs = low[:, 2, 400:401]
        entp = low[:, 2, 0:NCH * (TOP + 2)].rearrange("p (c g k) -> p c g k", c=CH, g=GT)
        nps = sums[:, 0:GT * (F + 1)].rearrange("p (t f) -> p t f", t=GT)
        whp = kbank[:, 0:GT * VF].rearrange("p (t f) -> p t f", t=GT)
        wps = work[:, :, :].rearrange("p a b -> p (a b)").rearrange("p (t e) -> p t e", t=GT)
        pps = [work, low]

        in_small = sem("in_small")
        in_x = sem("in_x")
        in_ent = sem("in_ent")
        adj_in = [sem(f"adj_in{k}") for k in range(GT)]
        edges_ready = sem("edges_ready")
        codes_done = sem("codes_done")
        codes_copied = sem("codes_copied")
        keyps_ready = sem("keyps_ready")
        keys_copied = sem("keys_copied")
        keys_used = sem("keys_used")
        cnt_ready = sem("cnt_ready")
        offs_ready = sem("offs_ready")
        expand_ready = sem("expand_ready")
        entries_ready = sem("entries_ready")
        idx_ready = sem("idx_ready")
        idx_copied = sem("idx_copied")
        ready = sem("const_ready")
        pe_pre = sem("pe_pre")
        dve_pre = sem("dve_pre")
        sum_ready = sem("sum_ready")
        sum_copied = sem("sum_copied")
        tab_out = sem("tab_out")
        h1_ready = sem("h1_ready")
        h1t_ready = sem("h1t_ready")
        h1t_copied = sem("h1t_copied")
        wh_ready = sem("wh_ready")
        v1_copied = sem("v1_copied")
        row_done = sem("row_done")
        out_ready = sem("out_ready")
        stored = [sem("stored0"), sem("stored1")]
        over_ready = sem("over_ready")
        overT_ready = sem("overT_ready")
        flag_ready = sem("flag_ready")
        rows_in = [[sem(f"rows_in{L}{k}") for k in range(2)] for L in range(2)]

        def pair(name):
            return [sem(f"{name}_l0"), sem(f"{name}_l1")]

        wt_ready, wps_ready, bias_ready, exps_done = pair("wt_ready"), pair("wps_ready"), pair("bias_ready"), pair("exps_done")
        p_ready, pps_ready, pt_ready, nv_done = pair("p_ready"), pair("pps_ready"), pair("pt_ready"), pair("nv_done")
        neg_ready, elu_done = pair("neg_ready"), pair("elu_done")
        link_pre, link_b1, link_b2, link_b3 = sem("link_pre"), sem("link_b1"), sem("link_b2"), sem("link_b3")
        link_t2, link_t4a, link_t4b = pair("link_t2"), pair("link_t4a"), pair("link_t4b")
        link_end = sem("link_end")
        passed = sem("passed")

        def alone(eng):
            eng.sem_inc(passed, 1)

        def linker(eng, semaphore, q=0, per=0):
            n = [0]

            def link(ins):
                n[0] += 1
                ins.then_inc(semaphore, 1)
                eng.wait_ge(semaphore, q * per + n[0])

            def check():
                assert not per or n[0] == per, (n[0], per)
            link.check = check
            return link

        def bc(ap, axis, n):
            v = ap.unsqueeze(axis)
            shape = list(v.shape)
            shape[axis] = n
            return v.broadcast_to(shape)

        def at(buf, q, n=GT):
            if isinstance(q, int):
                return buf[:, q * n:(q + 1) * n]
            return buf[:, bass.ds(q * n, n)]

        def at3(buf, q, lo, hi, n=GT):
            if isinstance(q, int):
                return buf[:, q * n:(q + 1) * n, lo:hi]
            return buf[:, bass.ds(q * n, n), lo:hi]

        def positive(eng, semaphore, value):
            if not isinstance(value, int) or value > 0:
                eng.wait_ge(semaphore, value)

        def rolled(eng, first, last, body, peel):
            for v in range(first, first + peel):
                body(v, v % 2)
            mid = first + peel
            pairs = max(0, (min(last, GROUPS) - mid) // 2)
            assert mid % 2 == 0
            if pairs:
                with eng.Fori(mid // 2, mid // 2 + pairs) as i:
                    body(i * 2, 0)
                    body(i * 2 + 1, 1)
            for v in range(mid + 2 * pairs, last):
                body(v, v % 2)

        LAG_B, LAG_T = 1, 2
        STEPS = GROUPS + LAG_T

        def has(v, lag):
            return not isinstance(v, int) or 0 <= v - lag < GROUPS

        block_ctx = ExitStack()
        block = block_ctx.enter_context(nc.Block())

        @block.sync
        def _(sp):
            sp.dma_start(cst[:, :], consts[:, :]).then_inc(in_small, 16)
            sp.dma_start(place_f[:, :], places[:, :]).then_inc(in_small, 16)
            sp.dma_start(W0s[:, :], W0[:, :]).then_inc(in_small, 16)
            for c in range(2):
                sp.dma_start(a0s[:, c:c + 1], a0[c * F:(c + 1) * F, :]).then_inc(in_small, 16)
            sp.dma_start(W1e[:, 0:F], W1[:, :]).then_inc(in_small, 16)
            for c in range(2):
                sp.dma_start(a1s[:, c:c + 1], a1[c * F:(c + 1) * F, :]).then_inc(in_small, 16)
            sp.dma_start(V[0][:, :, 0:F], ent_v).then_inc(in_ent, 16)
            for k in range(GT):
                sp.dma_start(A[:, k, :], adj[k * P:(k + 1) * P, :]).then_inc(adj_in[k], 16)
                if k == 0:
                    sp.dma_start(xs[:, :, :], x_v).then_inc(in_x, 16)
            with sp.Fori(1, GROUPS) as q:
                for k in range(GT):
                    sp.wait_ge(edges_ready, q * GT + (k + 1 - GT))
                    sp.dma_start(A[:, k, :], adj[bass.ds(q * (GT * P) + k * P, P), :]).then_inc(adj_in[k], 16)

        @block.gpsimd
        def _(pool):
            nc.gpsimd.memset(ones[:, :], 1.0).then_inc(ready, 1)
            nc.gpsimd.memset(ones2[:, :], 1.0).then_inc(ready, 1)
            nc.gpsimd.memset(V[0][:, :, F:F + 1], 1.0).then_inc(ready, 1)
            nc.gpsimd.memset(V[1][:, :, F:F + 1], 1.0).then_inc(ready, 1)

            def gather(L, q, k):
                if L == 0:
                    pool.wait_ge(idx_ready, q + 1)
                positive(pool, nv_done[L], q - 1)
                if L == 1:
                    if not isinstance(q, int) or q >= 2:
                        pool.wait_ge(rows_in[1][k], (q - k) * (NCH * 8))
                nc.gpsimd.tensor_copy(idx[k][:, :], at(idx_all, q, NCH)).then_inc(idx_copied, 1)
                pool.wait_ge(idx_copied, L * GROUPS + q + 1)
                alone(pool)
                for c in range(NCH):
                    nc.gpsimd.indirect_dma_start(
                        out=Vg[k][:, c, :], out_offset=None, in_=tab[L][:, :],
                        in_offset=bass.IndirectOffsetOnAxis(ap=idx[k][:, c:c + 1], axis=0),
                    ).then_inc(rows_in[L][k], 16)

            pool.wait_ge(tab_out, 16)
            rolled(pool, 0, GROUPS, lambda q, k: gather(0, q, k), 2)
            pool.wait_ge(tab_out, 16 * (1 + GROUPS))
            rolled(pool, 0, GROUPS, lambda q, k: gather(1, q, k), 2)

        def pe_scores(pe, L, q):
            pe.wait_ge(wt_ready[L], q + 1)
            for t in range(GT):
                for c in range(CH):
                    last = nc.tensor.transpose(wps[:, t, c * P:(c + 1) * P], wT[:, c * GT + t, :], ident)
            last.then_inc(wps_ready[L], 1)

        def pe_probs(pe, L, q):
            pe.wait_ge(p_ready[L], q + 1)
            for t in range(GT):
                for c in range(CH):
                    last = nc.tensor.transpose(pps[L][:, c, t * P:(t + 1) * P], E1[:, t, c * P:(c + 1) * P], ident)
            last.then_inc(pps_ready[L], 1)

        def pe_values(pe, L, q, k):
            pe.wait_ge(pt_ready[L], q + 1)
            for t in range(GT):
                for c in range(CH):
                    last = nc.tensor.matmul(nps[:, t, :], PT[:, c * GT + t, :], Vg[k][:, c * GT + t, 0:F + 1],
                                            start=(c == 0), stop=(c == CH - 1))
            last.then_inc(nv_done[L], 1)

        @block.tensor
        def _(pe):
            pe.wait_ge(in_small, 128)
            pe.wait_ge(ready, 4)
            nc.tensor.transpose(sums[0:F, 0:F], W0s[:, :], ident[0:F, 0:F])
            nc.tensor.transpose(sums[0:F, F:2 * F], W1e[:, 0:F], ident[0:F, 0:F]).then_inc(pe_pre, 1)
            pe.wait_ge(dve_pre, 1)
            for c in range(2):
                nc.tensor.matmul(sums[:, 128 + c * F:128 + (c + 1) * F], a0b[:, c, :], W0T[:, :], start=True, stop=True)
            nc.tensor.matmul(sums[0:F, 256:258], W1T[:, :], a1s[:, :], start=True, stop=True).then_inc(pe_pre, 1)
            pe.wait_ge(in_ent, 16)
            for t in range(TILES):
                last = nc.tensor.matmul(kbank[:, 0:F + 1], ones[:, :], V[0][:, t, 0:F + 1],
                                        start=(t == 0), stop=(t == TILES - 1))
            last.then_inc(sum_ready, 1)
            pe.wait_ge(dve_pre, 2)
            pe.wait_ge(sum_copied, 1)

            def tile_codes(q, k):
                pe.wait_ge(edges_ready, q * GT + k + 1)
                positive(pe, codes_copied, q * GT + (k + 1 - 2))
                for b in range(TILES):
                    last = nc.tensor.matmul(low[:, k % 2, b * CODES:(b + 1) * CODES],
                                            edges[:, k % 2, b * P:(b + 1) * P], code_w[:, :], start=True, stop=True)
                last.then_inc(codes_done, 1)

            def offsets(q):
                pe.wait_ge(cnt_ready, q + 1)
                nc.tensor.matmul(offs, before[:, :], cntb[:, :], start=True, stop=True).then_inc(offs_ready, 1)

            def entry_list(q):
                pe.wait_ge(expand_ready, q + 1)
                for c in range(CH):
                    last = nc.tensor.matmul(entp[:, c, :, :], R[:, c * P:(c + 1) * P], Xbd[:, :, :],
                                            start=True, stop=True)
                last.then_inc(entries_ready, 1)

            def key_pieces(q):
                pe.wait_ge(codes_copied, (q + 1) * GT)
                if not isinstance(q, int) or q >= 2:
                    pe.wait_ge(v1_copied, q - 1)
                for n, g0 in enumerate(range(0, CODES, 4)):
                    m = min(4, CODES - g0)
                    positive(pe, keys_copied, q * 3 + n)
                    nc.tensor.matmul(kbank[:, 0:m * P], ones2[:, :], place_w[:, g0 * P:(g0 + m) * P],
                                     start=True, stop=False)
                    for g in range(m):
                        last = nc.tensor.matmul(kbank[:, g * P:(g + 1) * P],
                                                codes[:, g0 + g, :, :].rearrange("p a b -> p (a b)"), ident,
                                                start=False, stop=(g == m - 1))
                    last.then_inc(keyps_ready, 1)

            def hidden_t(q):
                pe.wait_ge(h1_ready, q + 1)
                alone(pe)
                for t in range(GT):
                    last = nc.tensor.transpose(sums[0:F, t * P:(t + 1) * P], h1[:, t, :], ident)
                last.then_inc(h1t_ready, 1)

            def hidden_w(q):
                pe.wait_ge(h1t_copied, q + 1)
                pe.wait_ge(keys_copied, min(3 * (q + 2), 3 * GROUPS) if isinstance(q, int) else 3 * (q + 2))
                for t in range(GT):
                    last = nc.tensor.matmul(whp[:, t, :], h1T[:, t, :], W1e[:, :], start=True, stop=True)
                last.then_inc(wh_ready, 1)

            def step(v, k):
                if has(v, LAG_T):
                    pe_scores(pe, 0, v - LAG_T)
                if has(v, 0):
                    tile_codes(v, 0)
                if has(v, LAG_B):
                    offsets(v - LAG_B)
                if has(v, 0):
                    tile_codes(v, 1)
                if has(v, LAG_B):
                    entry_list(v - LAG_B)
                if has(v, LAG_T):
                    pe_probs(pe, 0, v - LAG_T)
                if has(v, 0):
                    tile_codes(v, 2)
                if has(v, LAG_T):
                    pe_values(pe, 0, v - LAG_T, k)
                if has(v, 0):
                    tile_codes(v, 3)
                if has(v, LAG_T):
                    hidden_t(v - LAG_T)
                    hidden_w(v - LAG_T)
                if has(v, 0):
                    key_pieces(v)

            rolled(pe, 0, STEPS, step, 2)
            pe.wait_ge(v1_copied, GROUPS)
            for t in range(TILES):
                last = nc.tensor.matmul(kbank[:, 0:F + 1], ones[:, :], V[1][:, t, 0:F + 1],
                                        start=(t == 0), stop=(t == TILES - 1))
            last.then_inc(sum_ready, 1)
            pe.wait_ge(over_ready, 1)
            nc.tensor.matmul(sums[0:1, 384:512], over[:, 1:2], ident, start=True, stop=True).then_inc(overT_ready, 1)
            pe.wait_ge(flag_ready, 1)

            def step1(v, k):
                if isinstance(v, int) and v >= GROUPS:
                    pe_values(pe, 1, v - 1, 1 - k)
                    return
                pe_scores(pe, 1, v)
                if not isinstance(v, int) or v >= 1:
                    pe_values(pe, 1, v - 1, 1 - k)
                pe_probs(pe, 1, v)

            rolled(pe, 0, GROUPS + 1, step1, 2)

        def act_exps(act, L, q):
            act.wait_ge(bias_ready[L], q + 1)
            for t in range(GT):
                nc.scalar.activation(E1[:, t, :], wps[:, t, :], ACT.Exp, bias=bias1[:, t:t + 1])
                last = nc.scalar.activation(E2[:, t, :], wps[:, t, :], ACT.Exp, bias=bias2[:, t:t + 1], scale=SLOPE)
            last.then_inc(exps_done[L], 1)

        def act_probs(act, L, q):
            act.wait_ge(pps_ready[L], q + 1)
            positive(act, nv_done[L], q)
            for c in range(CH):
                last = nc.scalar.copy(PT[:, c * GT:(c + 1) * GT, :],
                                      pps[L][:, c, :].rearrange("p (t r) -> p t r", t=GT))
            last.then_inc(pt_ready[L], 1)

        def act_elu(act, L, q):
            act.wait_ge(neg_ready[L], q + 1)
            nc.scalar.activation(en[:, :, :], neg[:, :, :], ACT.Exp).then_inc(elu_done[L], 1)

        @block.scalar
        def _(act):
            act.wait_ge(sum_ready, 1)
            nc.scalar.copy(sumV[0][:, :], kbank[:, 0:F + 1]).then_inc(sum_copied, 1)
            act.wait_ge(row_done, 1)
            act.dma_start(tab_v[0], V[0][:, :, :]).then_inc(tab_out, 16)

            def copy_codes(q, k):
                act.wait_ge(codes_done, q * GT + k + 1)
                if k == 0:
                    positive(act, keyps_ready, q * 3)
                nc.scalar.copy(codes[:, :, k, :],
                               low[:, k % 2, 0:TILES * CODES].rearrange("p (b c) -> p c b", c=CODES)
                               ).then_inc(codes_copied, 1)

            def copy_keys(q):
                for n, g0 in enumerate(range(0, CODES, 4)):
                    m = min(4, CODES - g0)
                    act.wait_ge(keyps_ready, q * 3 + (n + 1))
                    if n == 0:
                        positive(act, keys_used, q)
                    nc.scalar.copy(keys[:, g0 * P:(g0 + m) * P], kbank[:, 0:m * P]).then_inc(keys_copied, 1)

            def copy_hidden(q):
                act.wait_ge(h1t_ready, q + 1)
                nc.scalar.copy(h1T[:, :, :], sums[0:F, :].rearrange("p (t r) -> p t r", t=GT)).then_inc(h1t_copied, 1)

            def copy_values(q):
                act.wait_ge(wh_ready, q + 1)
                nc.scalar.copy(at3(V[1], q, 0, F), whp[:, :, 0:F])
                nc.scalar.copy(at(s[1], q), whp[:, :, F])
                nc.scalar.copy(at3(V[1], q, F + 1, F + 2), whp[:, :, F + 1:F + 2]).then_inc(v1_copied, 1)
                act.wait_ge(v1_copied, q + 1)
                if isinstance(q, int):
                    dst = tab_v[1][:, q * GT:(q + 1) * GT, :]
                else:
                    dst = tab_v[1][:, bass.ds(q * GT, GT), :]
                act.dma_start(dst, at3(V[1], q, 0, VF)).then_inc(tab_out, 16)

            def step(v, k):
                if has(v, 0):
                    copy_codes(v, 0)
                if has(v, LAG_T):
                    act_exps(act, 0, v - LAG_T)
                if has(v, 0):
                    copy_codes(v, 1)
                if has(v, LAG_T):
                    act_probs(act, 0, v - LAG_T)
                if has(v, 0):
                    copy_codes(v, 2)
                if has(v, LAG_T):
                    act_elu(act, 0, v - LAG_T)
                if has(v, 0):
                    copy_codes(v, 3)
                if has(v, LAG_T):
                    copy_hidden(v - LAG_T)
                    copy_values(v - LAG_T)
                if has(v, 0):
                    copy_keys(v)

            rolled(act, 0, STEPS, step, 2)
            act.wait_ge(sum_ready, 2)
            nc.scalar.copy(sumV[1][:, :], kbank[:, 0:F + 1]).then_inc(sum_copied, 1)

            def step1(v, k):
                if not isinstance(v, int) or v >= 1:
                    act_elu(act, 1, v - 1)
                if not isinstance(v, int) or v < GROUPS:
                    act_exps(act, 1, v)
                    act_probs(act, 1, v)
                if not isinstance(v, int) or v >= 1:
                    act.wait_ge(out_ready, v)
                    q = v - 1
                    dst = out_v[:, q * GT:(q + 1) * GT, :] if isinstance(q, int) else out_v[:, bass.ds(q * GT, GT), :]
                    act.dma_start(dst, outs[1 - k][:, :, :]).then_inc(stored[1 - k], 16)

            rolled(act, 0, GROUPS + 1, step1, 2)
            for k in range(2):
                act.wait_ge(stored[k], 16 * (GROUPS // 2))

        LINKS_B1, LINKS_B2, LINKS_B3, LINKS_T2, LINKS_T4A, LINKS_T4B = 10, 3, 11, 5, 4, (11 + 3 * NEWTON, 1)

        def layernorm_relu(dve, link, src, dst, t, xc, sq, n):
            alone(dve)
            link(nc.vector.reduce_sum(t["sum"][:, :], src, X))
            link(nc.vector.tensor_scalar(t["nmean"][:, :], t["sum"][:, :], -1.0 / F, None, ALU.mult))
            link(nc.vector.tensor_tensor(xc, src, bc(t["nmean"][:, :], 2, F), ALU.add))
            link(nc.vector.tensor_tensor(sq, xc, xc, ALU.mult))
            link(nc.vector.reduce_sum(t["ssq"][:, :], sq, X))
            link(nc.vector.tensor_scalar(t["var"][:, :], t["ssq"][:, :], 1.0 / F, EPS, ALU.mult, ALU.add))
            r, v = t["rstd"][:, :], t["var"][:, :]
            ri, g = r.bitcast(i32), t["ssq"][:, :]
            link(nc.vector.tensor_scalar(ri, v.bitcast(i32), 1, None, ALU.logical_shift_right))
            link(nc.vector.tensor_scalar(ri, ri, -1.0, float(0x5F3759DF), ALU.mult, ALU.add))
            for _ in range(NEWTON):
                link(nc.vector.tensor_tensor(g, r, r, ALU.mult))
                link(nc.vector.scalar_tensor_tensor(g, g, -0.5, v, ALU.mult, ALU.mult))
                link(nc.vector.scalar_tensor_tensor(r, g, 1.5, r, ALU.add, ALU.mult))
            link(nc.vector.tensor_scalar(xc, xc, 0.0, None, ALU.max))
            return nc.vector.tensor_tensor(dst, xc, bc(t["rstd"][:, :], 2, F), ALU.mult)

        def biases(link, L, q, sAP, n):
            link(nc.vector.tensor_scalar(Mc[:, 0:n], Mx[:, 0:n], FLOOR, None, ALU.max))
            nc.vector.tensor_scalar(empty[:, 0:n], Mx[:, 0:n], FLOOR, None, ALU.is_lt)
            link(nc.vector.tensor_tensor(sM[:, 0:n], Mc[:, 0:n], sAP, ALU.add))
            link(nc.vector.scalar_tensor_tensor(guard[:, 0:n], sM[:, 0:n], SLOPE, sM[:, 0:n], ALU.mult, ALU.max))
            link(nc.vector.tensor_tensor(bias1[:, 0:n], sAP, guard[:, 0:n], ALU.subtract))
            return nc.vector.scalar_tensor_tensor(bias2[:, 0:n], sAP, SLOPE, guard[:, 0:n], ALU.mult, ALU.subtract)

        def dve_masked(dve, L, q, k):
            dve.wait_ge(rows_in[L][k], (q - k + 2) * (NCH * 8))
            pq = pen[:, q, :, 0:P] if isinstance(q, int) else pen[:, bass.ds(q, 1), :, 0:P].rearrange("p a b c -> p (a b) c")
            nc.vector.tensor_tensor(wT[:, :, :], pq, Vg[k][:, :, F + 1:F + 2].broadcast_to([P, NCH, P]),
                                    ALU.add).then_inc(wt_ready[L], 1)

        def dve_guards(dve, L, q):
            link = linker(dve, link_t2[L], q, LINKS_T2)
            dve.wait_ge(wps_ready[L], q + 1)
            link(nc.vector.reduce_max(Mx[:, :], wps, X))
            biases(link, L, q, at(s[L], q), GT).then_inc(bias_ready[L], 1)
            link.check()

        def dve_weights(dve, L, q):
            dve.wait_ge(exps_done[L], q + 1)
            nc.vector.tensor_tensor(E1[:, :, :], E1[:, :, :], E2[:, :, :], ALU.max).then_inc(p_ready[L], 1)

        def attended(link, L, q, n, npsAP, tiles):
            link(nc.vector.tensor_tensor(att[:, 0:n, :], bc(sumV[L][:, :], 1, n),
                                         bc(empty[:, 0:n], 2, F + 1), ALU.mult))
            link(nc.vector.tensor_tensor(att[:, 0:n, :], att[:, 0:n, :], npsAP, ALU.add))
            link(nc.vector.reciprocal(rden[:, 0:n], att[:, 0:n, F]))
            last = nc.vector.tensor_tensor(hp[:, 0:n, :], att[:, 0:n, 0:F], bc(rden[:, 0:n], 2, F), ALU.mult)
            link(last)
            if L == 0:
                link(nc.vector.tensor_tensor(hp[:, 0:n, :], hp[:, 0:n, :], tiles(h0), ALU.add))
            return nc.vector.tensor_scalar(neg[:, 0:n, :], hp[:, 0:n, :], 0.0, None, ALU.min)

        def dve_attended(dve, L, q):
            link = linker(dve, link_t4a[L], q, LINKS_T4A + (L == 0))
            dve.wait_ge(nv_done[L], q + 1)
            attended(link, L, q, GT, nps, lambda b: at(b, q)).then_inc(neg_ready[L], 1)
            link.check()

        def dve_rows(dve, L, q, k):
            link = linker(dve, link_t4b[L], q, LINKS_T4B[L])
            dve.wait_ge(elu_done[L], q + 1)
            link(nc.vector.scalar_tensor_tensor(y[:, :, :], hp[:, :, :], 0.0, at(xs if L == 0 else x1, q),
                                                ALU.max, ALU.add))
            if L == 0:
                xq = at(x1, q)
                link(nc.vector.scalar_tensor_tensor(xq, en[:, :, :], -1.0, y[:, :, :], ALU.add, ALU.add))
                layernorm_relu(dve, link, xq, h1[:, :, :], ln, lnc[:, :, :], lnq[:, :, :], GT).then_inc(h1_ready, 1)
            else:
                if not isinstance(q, int) or q >= 2:
                    dve.wait_ge(stored[k], (q - k) * 8)
                nc.vector.scalar_tensor_tensor(outs[k][:, :, :], en[:, :, :], -1.0, y[:, :, :],
                                               ALU.add, ALU.add).then_inc(out_ready, 1)
            link.check()

        @block.vector
        def _(dve):
            link = linker(dve, link_pre)
            nc.vector.memset(over[:, :], 0.0)
            dve.wait_ge(in_small, 128)
            nc.vector.tensor_copy(code_w[:, :], cst[:, where["code"][0]:where["code"][1]])
            nc.vector.tensor_copy(before[:, :], cst[:, where["before"][0]:where["before"][1]])
            nc.vector.tensor_copy(bit_w[:, :], cst[:, where["bit"][0]:where["bit"][1]])
            nc.vector.tensor_copy(kept[:, TOP + 1:TOP + 2], cst[:, where["block"][0]:where["block"][1]])
            nc.vector.tensor_copy(place_w[:, :], place_f[:, :])
            nc.vector.tensor_copy(a0b[:, :, :], a0s[:, :].unsqueeze(2).broadcast_to([F, 2, P]))
            dve.wait_ge(pe_pre, 1)
            nc.vector.tensor_copy(W0T[:, :], sums[0:F, 0:F])
            nc.vector.tensor_copy(W1T[:, :], sums[0:F, F:2 * F]).then_inc(dve_pre, 1)
            dve.wait_ge(pe_pre, 2)
            nc.vector.tensor_copy(W1e[:, F:F + 2], sums[0:F, 256:258])
            nc.vector.tensor_copy(wbc[:, :, :], sums[:, 128:256].rearrange("p (c f) -> p c f", c=2)
                                  ).then_inc(dve_pre, 1)
            dve.wait_ge(dve_pre, 2)
            dve.wait_ge(in_ent, 16)
            link(nc.vector.tensor_tensor(lnc0, V[0][:, :, 0:F], bc(wbc[:, 1, :], 1, TILES), ALU.mult))
            nc.vector.reduce_sum(V[0][:, :, F + 1], lnc0, X).then_inc(row_done, 1)
            dve.wait_ge(in_x, 16)
            link(layernorm_relu(dve, link, xs[:, :, :], h0[:, :, :], ln0, lnc0, lnq0, TILES))
            link(nc.vector.tensor_tensor(lnc0, h0[:, :, :], bc(wbc[:, 0, :], 1, TILES), ALU.mult))
            link(nc.vector.reduce_sum(s[0][:, :], lnc0, X))

            def tile_edges(q, k):
                dve.wait_ge(adj_in[k], (q + 1) * 16)
                positive(dve, codes_done, q * GT + (k + 1 - 2))
                nc.vector.tensor_scalar(edges[:, k % 2, :], A[:, k, :], 0.0, None, ALU.is_gt).then_inc(edges_ready, 1)

            def best_keys(q):
                link = linker(dve, link_b1, q, LINKS_B1)
                dve.wait_ge(keys_copied, q * 3 + 3)
                alone(dve)
                for n in range(NSEG):
                    last = nc.vector.max(slots[:, n, :], keys[:, n * SEG:(n + 1) * SEG])
                last.then_inc(keys_used, 1)
                dve.wait_ge(keys_used, q + 1)
                link(nc.vector.reduce_max(over[:, 1:2], slots[:, :, 7], X))
                flat = slots[:, :, :].rearrange("p a b -> p (a b)")
                for r in range(TOP // 8):
                    alone(dve)
                    link(nc.vector.max(top[:, 8 * r:8 * r + 8], flat))
                    if r < TOP // 8 - 1:
                        alone(dve)
                        link(nc.vector.match_replace(flat, top[:, 8 * r:8 * r + 8], flat, 0.0))
                nc.vector.tensor_tensor(over[:, 2:3], over[:, 1:2], top[:, TOP - 1:TOP], ALU.max)
                link(nc.vector.tensor_scalar(isv[:, :], top[:, :], VALID, None, ALU.is_ge))
                link(nc.vector.reduce_sum(cnt[:, :], isv[:, :], X))
                link(nc.vector.tensor_tensor(over[:, 0:1], over[:, 0:1], over[:, 2:3], ALU.max))
                link(nc.vector.tensor_tensor(kept[:, 0:TOP], top[:, :], isv[:, :], ALU.mult))
                nc.vector.tensor_copy(cntb[:, :], cnt[:, :]).then_inc(cnt_ready, 1)
                link.check()

            def expand(q):
                link = linker(dve, link_b2, q, LINKS_B2)
                dve.wait_ge(offs_ready, q + 1)
                nc.vector.tensor_copy(kept[:, TOP:TOP + 1], offs)
                link(nc.vector.tensor_tensor(end[:, :], cnt[:, :], offs, ALU.add))
                nc.vector.tensor_scalar(R0[:, :], slot_no, kept[:, TOP:TOP + 1], None, ALU.is_ge)
                link(nc.vector.tensor_scalar(over[:, 3:4], end[:, :], float(ENTRIES), 2.0 * VALID, ALU.is_gt, ALU.mult))
                link(nc.vector.tensor_tensor(over[:, 0:1], over[:, 0:1], over[:, 3:4], ALU.max))
                nc.vector.tensor_tensor(Xbd[:, :, :], bc(kept[:, :], 1, GT), bc(tile_of, 2, TOP + 2), ALU.mult)
                nc.vector.scalar_tensor_tensor(R[:, :], slot_no, end[:, 0:1], R0[:, :],
                                               ALU.is_lt, ALU.mult).then_inc(expand_ready, 1)
                link.check()

            def decode(q):
                link = linker(dve, link_b3, q, LINKS_B3)
                dve.wait_ge(entries_ready, q + 1)
                d3 = dist[:, :].rearrange("p (c g) -> p c g", c=CH)
                link(nc.vector.tensor_tensor(d3, bc(entry_no, 2, GT), entp[:, :, :, TOP], ALU.subtract))
                link(nc.vector.tensor_tensor(hit[:, :, :], bc(top_no, 1, NCH), bc(dist[:, :], 2, TOP), ALU.is_equal))
                e3 = entp.rearrange("p c g k -> p (c g) k")
                link(nc.vector.tensor_tensor(hit[:, :, :], hit[:, :, :], e3[:, :, 0:TOP], ALU.mult))
                link(nc.vector.reduce_sum(dist[:, :], hit[:, :, :], X))
                link(nc.vector.tensor_copy(keyi[:, :], dist[:, :]))
                nc.vector.tensor_scalar(grp[:, :], keyi[:, :], 7, 15, ALU.logical_shift_right, ALU.bitwise_and)
                nc.vector.tensor_scalar(col[:, :], keyi[:, :], 127, None, ALU.bitwise_and)
                link(nc.vector.tensor_scalar(code[:, :], keyi[:, :], POSBITS, None, ALU.logical_shift_right))
                link(nc.vector.tensor_tensor(biti[:, :, :], bc(code[:, :], 2, ROWS), bc(bit_w[:, :], 1, NCH),
                                             ALU.bitwise_and))
                nc.vector.scalar_tensor_tensor(at(idx_all, q, NCH), e3[:, :, TOP + 1], float(P), col[:, :],
                                               ALU.mult, ALU.add).then_inc(idx_ready, 1)
                link(nc.vector.tensor_scalar(bitb[:, :, :], biti[:, :, :], 0.0, None, ALU.is_gt))
                link(nc.vector.tensor_tensor(grpb[:, :, :], bc(group_no, 1, NCH), bc(grp[:, :], 2, CODES),
                                             ALU.is_equal))
                m4 = mask[:, :, :].rearrange("p n (c r) -> p n c r", c=CODES)
                link(nc.vector.tensor_tensor(m4, bc(grpb[:, :, :], 3, ROWS), bc(bitb[:, :, :], 2, CODES), ALU.mult))
                pq = pen[:, q, :, :] if isinstance(q, int) else pen[:, bass.ds(q, 1), :, :].rearrange("p a b c -> p (a b) c")
                link(nc.vector.tensor_scalar(pq, mask[:, :, :], BIG, -BIG, ALU.mult, ALU.add))
                link.check()

            def step(v, k):
                if has(v, LAG_T):
                    dve_masked(dve, 0, v - LAG_T, k)
                if has(v, 0):
                    tile_edges(v, 0)
                if has(v, LAG_B):
                    best_keys(v - LAG_B)
                if has(v, LAG_T):
                    dve_guards(dve, 0, v - LAG_T)
                if has(v, 0):
                    tile_edges(v, 1)
                if has(v, LAG_B):
                    expand(v - LAG_B)
                if has(v, LAG_T):
                    dve_weights(dve, 0, v - LAG_T)
                if has(v, 0):
                    tile_edges(v, 2)
                if has(v, LAG_B):
                    decode(v - LAG_B)
                if has(v, LAG_T):
                    dve_attended(dve, 0, v - LAG_T)
                if has(v, 0):
                    tile_edges(v, 3)
                if has(v, LAG_T):
                    dve_rows(dve, 0, v - LAG_T, k)

            rolled(dve, 0, STEPS, step, 2)
            nc.vector.tensor_copy(over[:, 1:2], over[:, 0:1]).then_inc(over_ready, 1)
            link = linker(dve, link_end)
            dve.wait_ge(overT_ready, 1)
            link(nc.vector.reduce_max(end[0:1, :], sums[0:1, 384:512], X))
            nc.vector.tensor_scalar(flag[:, :], end[0:1, :], VALID, None, ALU.is_ge).then_inc(flag_ready, 1)
            dve.wait_ge(sum_copied, 2)

            def step1(v, k):
                run = not isinstance(v, int) or v < GROUPS
                fin = not isinstance(v, int) or v >= 1
                if run:
                    dve_masked(dve, 1, v, k)
                if fin:
                    dve_attended(dve, 1, v - 1)
                if run:
                    dve_guards(dve, 1, v)
                if fin:
                    dve_rows(dve, 1, v - 1, 1 - k)
                if run:
                    dve_weights(dve, 1, v)

            rolled(dve, 0, GROUPS + 1, step1, 2)

        block_ctx.close()
        block_ctx = ExitStack()
        block = block_ctx.enter_context(nc.Block())
        score = A[:, 1, :].bitcast(fp32)
        ex1 = A[:, 2, :].bitcast(fp32)
        ex2 = A[:, 3, :].bitcast(fp32)
        trow = edges[:, :, :].rearrange("p a b -> p (a b)").bitcast(fp32)
        diag = wT[:, 0, :]
        UNITS = TILES // 4
        g = {n: sem("g_" + n) for n in (
            "x_in", "adj_in", "score_ready", "diag_ready", "spread", "spread_copied", "sum_ready", "sum_copied",
            "bias_ready", "exps_done", "p_ready", "turned", "turned_copied", "values_done", "neg_ready",
            "elu_done", "h1_ready", "h1t_ready", "h1t_copied", "wh_ready", "v1_copied", "out_ready", "stored")}
        g_link = {n: sem("g_link_" + n) for n in ("a0", "a1", "b0", "b1", "c0", "c1")}

        def one(buf, t):
            return buf[:, t:t + 1] if isinstance(t, int) else buf[:, bass.ds(t, 1)]

        def one3(buf, t, lo, hi):
            return buf[:, t:t + 1, lo:hi] if isinstance(t, int) else buf[:, bass.ds(t, 1), lo:hi]

        def each_tile(eng, body, peel=0):
            for t in range(peel):
                body(t)
            with eng.Fori(peel, TILES) as t:
                body(t)

        def general(eng, program):
            with eng.If(eng.value_load(flag[0:1, 0:1], min_val=0, max_val=1) > 0):
                program()

        @block.sync
        def _(sp):
            def program():
                sp.dma_start(xs[:, :, :], x_v).then_inc(g["x_in"], 16)
                for L in range(2):
                    def tile(t):
                        if L or not isinstance(t, int):
                            sp.wait_ge(g["score_ready"], L * TILES + t)
                        sp.dma_start(A[:, 0, :], adj[bass.ds(t * P, P), :]).then_inc(g["adj_in"], 16)
                    each_tile(sp, tile, 1)
            general(sp, program)

        @block.tensor
        def _(pe):
            def program():
                for L in range(2):
                    if L:
                        pe.wait_ge(g["v1_copied"], TILES)
                        for t in range(TILES):
                            last = nc.tensor.matmul(kbank[:, 0:F + 1], ones[:, :], V[1][:, t, 0:F + 1],
                                                    start=(t == 0), stop=(t == TILES - 1))
                        last.then_inc(g["sum_ready"], 1)
                        pe.wait_ge(g["sum_copied"], 1)

                    def spread(t):
                        pe.wait_ge(g["diag_ready"], L * TILES + t + 1)
                        nc.tensor.matmul(kbank[:, 0:P], ones[:, :], diag, start=True, stop=True).then_inc(g["spread"], 1)
                    each_tile(pe, spread)

                    def turn(t, u):
                        if u == 0:
                            pe.wait_ge(g["p_ready"], L * TILES + t + 1)
                        if L or u or not isinstance(t, int):
                            if not (L == 0 and isinstance(t, int) and u < 2):
                                pe.wait_ge(g["turned_copied"], (L * TILES + t) * UNITS + (u - 1))
                        for b in range(4):
                            last = nc.tensor.transpose(work[:, u % 2, b * P:(b + 1) * P],
                                                       ex1[:, (4 * u + b) * P:(4 * u + b + 1) * P], ident)
                        last.then_inc(g["turned"], 1)

                    def values(t, u):
                        pe.wait_ge(g["turned_copied"], (L * TILES + t) * UNITS + (u + 1))
                        for b in range(4):
                            last = nc.tensor.matmul(nps[:, 0, :], PT[:, 4 * (u % 2) + b, :], V[L][:, 4 * u + b, 0:F + 1],
                                                    start=(u + b == 0), stop=(4 * u + b == TILES - 1))
                        last.then_inc(g["values_done"], 1)

                    def tile(t):
                        turn(t, 0)
                        for u in range(UNITS):
                            if u + 1 < UNITS:
                                turn(t, u + 1)
                            values(t, u)
                        if L == 0:
                            pe.wait_ge(g["h1_ready"], t + 1)
                            alone(pe)
                            nc.tensor.transpose(sums[0:F, P:2 * P], h1[:, 0, :], ident).then_inc(g["h1t_ready"], 1)
                            pe.wait_ge(g["h1t_copied"], t + 1)
                            nc.tensor.matmul(whp[:, 0, :], h1T[:, 0, :], W1e[:, :], start=True, stop=True
                                             ).then_inc(g["wh_ready"], 1)
                    each_tile(pe, tile, 1)
            general(pe, program)

        @block.scalar
        def _(act):
            def program():
                for L in range(2):
                    if L:
                        act.wait_ge(g["sum_ready"], 1)
                        nc.scalar.copy(sumV[1][:, :], kbank[:, 0:F + 1]).then_inc(g["sum_copied"], 1)

                    def spread(t):
                        act.wait_ge(g["spread"], L * TILES + t + 1)
                        nc.scalar.copy(trow[:, t * P:(t + 1) * P] if isinstance(t, int) else trow[:, bass.ds(t * P, P)],
                                       kbank[:, 0:P]).then_inc(g["spread_copied"], 1)
                    each_tile(act, spread)

                    def tile(t):
                        act.wait_ge(g["bias_ready"], L * TILES + t + 1)
                        nc.scalar.activation(ex1, score, ACT.Exp, bias=bias1[:, 0:1])
                        nc.scalar.activation(ex2, score, ACT.Exp, bias=bias2[:, 0:1], scale=SLOPE
                                             ).then_inc(g["exps_done"], 1)
                        for u in range(UNITS):
                            act.wait_ge(g["turned"], (L * TILES + t) * UNITS + (u + 1))
                            if not (L == 0 and isinstance(t, int) and u < 2):
                                act.wait_ge(g["values_done"], (L * TILES + t) * UNITS + (u - 1))
                            nc.scalar.copy(PT[:, 4 * (u % 2):4 * (u % 2) + 4, :],
                                           work[:, u % 2, :].rearrange("p (b r) -> p b r", b=4)
                                           ).then_inc(g["turned_copied"], 1)
                        act.wait_ge(g["neg_ready"], L * TILES + t + 1)
                        nc.scalar.activation(en[:, 0, :], neg[:, 0, :], ACT.Exp).then_inc(g["elu_done"], 1)
                        if L == 0:
                            act.wait_ge(g["h1t_ready"], t + 1)
                            nc.scalar.copy(h1T[:, 0, :], sums[0:F, P:2 * P]).then_inc(g["h1t_copied"], 1)
                            act.wait_ge(g["wh_ready"], t + 1)
                            nc.scalar.copy(one3(V[1], t, 0, F), whp[:, 0:1, 0:F])
                            nc.scalar.copy(one(s[1], t), whp[:, 0, F:F + 1])
                            nc.scalar.copy(one3(V[1], t, F + 1, F + 2), whp[:, 0:1, F + 1:F + 2]
                                           ).then_inc(g["v1_copied"], 1)
                        else:
                            act.wait_ge(g["out_ready"], t + 1)
                            act.dma_start(out[bass.ds(t * P, P), :], outs[0][:, 0, :]).then_inc(g["stored"], 16)
                    each_tile(act, tile, 1)
                act.wait_ge(g["stored"], 16 * TILES)
            general(act, program)

        @block.vector
        def _(dve):
            def program():
                dve.wait_ge(g["x_in"], 16)
                for L in range(2):
                    if L:
                        dve.wait_ge(g["v1_copied"], TILES)

                    def spread(t):
                        if L or not isinstance(t, int):
                            dve.wait_ge(g["spread_copied"], L * TILES + t)
                        nc.vector.tensor_scalar(diag, ident, one3(V[L], t, F + 1, F + 2).rearrange("p a b -> p (a b)"),
                                                None, ALU.mult).then_inc(g["diag_ready"], 1)
                    each_tile(dve, spread, 1)
                    dve.wait_ge(g["spread_copied"], (L + 1) * TILES)

                    def tile(t):
                        link = linker(dve, g_link[f"a{L}"], t, 7)
                        dve.wait_ge(g["adj_in"], (L * TILES + t + 1) * 16)
                        nc.vector.tensor_scalar(score, A[:, 0, :], 0.0, -BIG, ALU.is_le, ALU.mult
                                                ).then_inc(g["score_ready"], 1)
                        dve.wait_ge(g["score_ready"], L * TILES + t + 1)
                        link(nc.vector.tensor_tensor(score, score, trow, ALU.add))
                        link(nc.vector.reduce_max(Mx[:, 0:1], score, X))
                        link(nc.vector.tensor_copy(sT, one(s[L], t)))
                        biases(link, L, t, sT, 1).then_inc(g["bias_ready"], 1)
                        link.check()
                        dve.wait_ge(g["exps_done"], L * TILES + t + 1)
                        nc.vector.tensor_tensor(ex1, ex1, ex2, ALU.max).then_inc(g["p_ready"], 1)
                        link = linker(dve, g_link[f"b{L}"], t, LINKS_T4A + (L == 0))
                        dve.wait_ge(g["values_done"], (L * TILES + t + 1) * UNITS)
                        attended(link, L, t, 1, nps[:, 0:1, :], lambda b: one3(b, t, 0, F)).then_inc(g["neg_ready"], 1)
                        link.check()
                        link = linker(dve, g_link[f"c{L}"], t, LINKS_T4B[L])
                        dve.wait_ge(g["elu_done"], L * TILES + t + 1)
                        link(nc.vector.scalar_tensor_tensor(y[:, 0:1, :], hp[:, 0:1, :], 0.0, one3(xs, t, 0, F),
                                                            ALU.max, ALU.add))
                        if L == 0:
                            link(nc.vector.scalar_tensor_tensor(one3(xs, t, 0, F), en[:, 0:1, :], -1.0, y[:, 0:1, :],
                                                                ALU.add, ALU.add))
                            layernorm_relu(dve, link, one3(xs, t, 0, F), h1[:, 0:1, :], {k: v[:, 0:1] for k, v in ln.items()},
                                           lnc[:, 0:1, :], lnq[:, 0:1, :], 1).then_inc(g["h1_ready"], 1)
                        else:
                            if not isinstance(t, int):
                                dve.wait_ge(g["stored"], t * 16)
                            nc.vector.scalar_tensor_tensor(outs[0][:, 0:1, :], en[:, 0:1, :], -1.0, y[:, 0:1, :],
                                                           ALU.add, ALU.add).then_inc(g["out_ready"], 1)
                        link.check()
                    each_tile(dve, tile, 1)
            general(dve, program)
        block_ctx.close()


_INS = ['x', 'adj', 'L0_gnn_entity_embs', 'L0_gnn_W', 'L0_gnn_a', 'L1_gnn_W', 'L1_gnn_a']
_OUTS = [((4096, 64), 'float32')]


def shape_constants():
    import numpy as np

    where, width = const_columns()
    c = np.zeros((P, width), np.float32)
    p = np.arange(P)

    def put(name, v):
        c[:, where[name][0]:where[name][1]] = v

    put("ident", np.eye(P))
    off = p[:, None] - ROWS * np.arange(CODES)[None, :]
    put("code", np.where((off >= 0) & (off < ROWS), VALID * 2.0 ** np.clip(off, 0, ROWS), 0.0))
    put("before", (p[:, None] < p[None, :]) & (p[:, None] // TILES == p[None, :] // TILES))
    put("tile", p[:, None] // TILES == np.arange(GT)[None, :])
    put("block", (p % TILES)[:, None])
    put("slot", np.arange(ENTRIES)[None, :])
    put("entry", p[:, None] + P * np.arange(CH)[None, :])
    put("top", np.arange(TOP)[None, :])
    put("group", np.arange(CODES)[None, :])
    put("bit", 2.0 ** np.arange(ROWS)[None, :])
    pos = np.arange(POS)
    return c, np.stack([pos // P * P, pos % P]).astype(np.float32)


def kernel(**inputs):
    import numpy as _np
    import concourse.bacc as _bacc
    from concourse import mybir as _mybir
    from concourse.bass_utils import run_bass_kernel_spmd as _run

    nc = _bacc.Bacc("TRN2", target_bir_lowering=False, num_devices=1)
    arrays, args = {}, []

    def add(name, a):
        arrays[name] = a
        args.append(nc.dram_tensor(name, a.shape, _mybir.dt.from_np(a.dtype), kind="ExternalInput").ap())

    for name in _INS:
        add(f"in_{name}_dram", _np.ascontiguousarray(inputs[name]))
    consts, places = shape_constants()
    add("const_tables_dram", consts)
    add("const_places_dram", places)
    for n in range(2):
        args.append(nc.dram_tensor(f"value_table{n}", (N, VF), _mybir.dt.float32, kind="Internal").ap())
    for i, (shape, dtype) in enumerate(_OUTS):
        dt = _mybir.dt.from_np(_np.dtype(dtype))
        args.append(nc.dram_tensor(f"out_{i}_dram", shape, dt, kind="ExternalOutput").ap())
    graph_attention(nc, *args)
    r = _run(nc, [arrays], core_ids=[0])
    return r.results[0]["out_0_dram"]
```

```python
import concourse.bass as bass
from concourse import mybir
from contextlib import ExitStack


N = 4096
F = 64
P = 128
TILES = N // P
GT = 4
GROUPS = TILES // GT
ROWS = 13
CODES = -(-P // ROWS)
POS = CODES * P
POSBITS = 11
VALID = float(1 << POSBITS)
SEG = 64
NSEG = POS // SEG
TOP = 24
CH = 3
ENTRIES = CH * P
NCH = CH * GT
VF = F + 2
MROWS = CODES * ROWS
BIG = 1.0e30
FLOOR = -1.0e20
SLOPE = 0.2
EPS = 1e-5
NEWTON = 3


def const_columns():
    at, where = 0, {}
    for name, width in (("ident", P), ("code", CODES), ("before", P), ("tile", GT), ("block", 1),
                        ("slot", ENTRIES), ("entry", CH), ("top", TOP), ("group", CODES), ("bit", ROWS)):
        where[name] = (at, at + width)
        at += width
    return where, at


def graph_attention(nc, x, adj, ent, W0, a0, W1, a1, consts, places, tab0, tab1, out):
    fp32 = mybir.dt.float32
    bf16 = mybir.dt.bfloat16
    i32 = mybir.dt.int32
    ALU = mybir.AluOpType
    ACT = mybir.ActivationFunctionType
    X = mybir.AxisListType.X
    where, width = const_columns()

    x_v = x.rearrange("(t p) f -> p t f", p=P)
    out_v = out.rearrange("(t p) f -> p t f", p=P)
    ent_v = ent.rearrange("(t p) f -> p t f", p=P)
    tab_v = [t.rearrange("(t p) f -> p t f", p=P) for t in (tab0, tab1)]
    tab = [tab0, tab1]

    ctx = ExitStack()
    with ctx:
        def sb(name, shape, dt=fp32):
            return ctx.enter_context(nc.sbuf_tensor(name, shape, dt))

        def ps(name, shape):
            return ctx.enter_context(nc.psum_tensor(name, shape, fp32))

        def sem(name):
            return ctx.enter_context(nc.semaphore(name))

        cst = sb("cst", [P, width])
        ident = cst[:, where["ident"][0]:where["ident"][1]]
        tile_of = cst[:, where["tile"][0]:where["tile"][1]]
        slot_no = cst[:, where["slot"][0]:where["slot"][1]]
        entry_no = cst[:, where["entry"][0]:where["entry"][1]]
        top_no = cst[:, where["top"][0]:where["top"][1]]
        group_no = cst[:, where["group"][0]:where["group"][1]]
        code_w = sb("code_w", [P, CODES], bf16)
        before = sb("before", [P, P], bf16)
        bit_w = sb("bit_w", [P, ROWS], i32)
        place_w = sb("place_w", [2, POS], bf16)
        ones2 = sb("ones2", [2, P], bf16)
        ones = sb("ones", [P, P])
        W0s = sb("W0s", [F, F])
        W0T = sb("W0T", [F, F])
        a0s = sb("a0s", [F, 2])
        a0b = sb("a0b", [F, 2, P])
        W1e = sb("W1e", [F, VF])
        W1T = sb("W1T", [F, F])
        a1s = sb("a1s", [F, 2])
        wbc = sb("wbc", [P, 2, F])
        xs = sb("xs", [P, TILES, F])
        h0 = sb("h0", [P, TILES, F])
        x1 = xs
        V = [sb("V0", [P, TILES, VF]), sb("V1", [P, TILES, VF])]
        s = [sb("s0", [P, TILES]), sb("s1", [P, TILES])]
        sumV = [sb("sumV0", [P, VF]), sb("sumV1", [P, VF])]
        A = sb("A", [P, GT, N], i32)
        edges = sb("edges", [P, 2, N], bf16)
        codes = sb("codes", [P, CODES, GT, TILES])
        keys = sb("keys", [P, POS])
        place_f = keys[0:2, :]
        slots = sb("slots", [P, NSEG, 8])
        top = sb("top", [P, TOP])
        over = sb("over", [P, 4])
        kept = sb("kept", [P, TOP + 2])
        isv = sb("isv", [P, TOP])
        cnt = sb("cnt", [P, 1])
        cntb = sb("cntb", [P, 1], bf16)
        end = sb("end", [P, 1])
        R = sb("R", [P, ENTRIES])
        Xbd = sb("Xbd", [P, GT, TOP + 2])
        dist = sb("dist", [P, NCH])
        hit = sb("hit", [P, NCH, TOP])
        keyi = sb("keyi", [P, NCH], i32)
        grp = sb("grp", [P, NCH], i32)
        col = sb("col", [P, NCH], i32)
        code = sb("code", [P, NCH], i32)
        biti = sb("biti", [P, NCH, ROWS], i32)
        bitb = sb("bitb", [P, NCH, ROWS], bf16)
        grpb = sb("grpb", [P, NCH, CODES], bf16)
        mask = sb("mask", [P, NCH, MROWS], bf16)
        R0 = mask[:, :, :].rearrange("p n m -> p (n m)").bitcast(fp32)[:, 0:ENTRIES]
        pen = sb("pen", [P, GROUPS, NCH, MROWS], bf16)
        idx_all = sb("idx_all", [P, GROUPS * NCH], i32)
        flag = sb("flag", [1, 1], i32)
        Vrows1 = A[:, 0:2, :].rearrange("p k n -> p (k n)").bitcast(fp32)[:, 0:GROUPS * NCH * VF].rearrange(
            "p (q c v) -> p q c v", q=GROUPS, c=NCH)
        Vg = [sb("Vga", [P, NCH, VF]), sb("Vgb", [P, NCH, VF])]
        wT = sb("wT", [P, NCH, P])
        E1 = sb("E1", [P, GT, ENTRIES])
        E2 = sb("E2", [P, GT, ENTRIES])
        PT = sb("PT", [P, NCH, P])
        Mx = sb("Mx", [P, GT])
        Mc = sb("Mc", [P, GT])
        sM = sb("sM", [P, GT])
        guard = sb("guard", [P, GT])
        bias1 = sb("bias1", [P, GT])
        bias2 = sb("bias2", [P, GT])
        empty = sb("empty", [P, 2, GT])
        att = sb("att", [P, GT, VF])
        rden = sb("rden", [P, GT])
        hp = sb("hp", [P, GT, F])
        neg = sb("neg", [P, GT, F])
        en = sb("en", [P, GT, F])
        y = sb("y", [P, GT, F])
        outs = [sb("outa", [P, GT, F]), sb("outb", [P, GT, F])]
        sT = dist[:, 0:1]
        h1 = sb("h1", [P, GT, F])
        h1T = sb("h1T", [F, GT, P])
        mean = sb("mean", [P, GT])
        nmean = sb("nmean", [P, GT])
        ssq = sb("ssq", [P, TILES])
        rstd = sb("rstd", [P, 3, TILES])
        big = pen[:, :, :, :].rearrange("p a b c -> p (a b c)").bitcast(fp32)
        lnc0 = big[:, 0:TILES * F].rearrange("p (t f) -> p t f", f=F)
        lnq0 = big[:, TILES * F:2 * TILES * F].rearrange("p (t f) -> p t f", f=F)

        low = ps("low", [P, 3, 512])
        sums = ps("sums", [P, 512])
        work = ps("work", [P, 3, 512])
        kbank = ps("kbank", [P, 512])
        offs = low[:, 2, 400:401]
        entp = low[:, 2, 0:NCH * (TOP + 2)].rearrange("p (c g k) -> p c g k", c=CH, g=GT)
        nps = sums[:, 0:GT * VF].rearrange("p (t f) -> p t f", t=GT)
        whp = kbank[:, 0:GT * VF].rearrange("p (t f) -> p t f", t=GT)
        wps = work[:, :, :].rearrange("p a b -> p (a b)").rearrange("p (t e) -> p t e", t=GT)
        pps = [work, low]

        in_small = sem("in_small")
        in_x = sem("in_x")
        in_ent = sem("in_ent")
        adj_in = [sem(f"adj_in{k}") for k in range(GT)]
        edges_ready = sem("edges_ready")
        codes_done = sem("codes_done")
        codes_copied = sem("codes_copied")
        keyps_ready = sem("keyps_ready")
        keys_copied = sem("keys_copied")
        keys_used = sem("keys_used")
        cnt_ready = sem("cnt_ready")
        offs_ready = sem("offs_ready")
        expand_ready = sem("expand_ready")
        entries_ready = sem("entries_ready")
        idx_ready = sem("idx_ready")
        ready = sem("const_ready")
        pe_pre = sem("pe_pre")
        dve_pre = sem("dve_pre")
        sum_ready = sem("sum_ready")
        sum_copied = sem("sum_copied")
        tab_out = sem("tab_out")
        mean_ready = sem("mean_ready")
        h1_ready = sem("h1_ready")
        h1t_ready = sem("h1t_ready")
        h1t_copied = sem("h1t_copied")
        wh_ready = sem("wh_ready")
        v1_copied = sem("v1_copied")
        v1_scaled = sem("v1_scaled")
        row_done = sem("row_done")
        out_ready = sem("out_ready")
        stored = [sem("stored0"), sem("stored1")]
        over_ready = sem("over_ready")
        overT_ready = sem("overT_ready")
        flag_ready = sem("flag_ready")
        rows_in = [[sem(f"rows_in{L}{k}") for k in range(2)] for L in range(2)]

        def pair(name):
            return [sem(f"{name}_l0"), sem(f"{name}_l1")]

        wt_ready, wps_ready, bias_ready, exps_done = pair("wt_ready"), pair("wps_ready"), pair("bias_ready"), pair("exps_done")
        p_ready, pps_ready, pt_ready, nv_done = pair("p_ready"), pair("pps_ready"), pair("pt_ready"), pair("nv_done")
        neg_ready, elu_done = pair("neg_ready"), pair("elu_done")
        link_pre, link_b1, link_b2, link_b3 = sem("link_pre"), sem("link_b1"), sem("link_b2"), sem("link_b3")
        link_t2, link_t4a, link_t4b = pair("link_t2"), pair("link_t4a"), pair("link_t4b")
        link_end = sem("link_end")
        link_sc = sem("link_sc")
        passed = sem("passed")

        def alone(eng):
            eng.sem_inc(passed, 1)

        def linker(eng, semaphore, q=0, per=0):
            n = [0]

            def link(ins):
                n[0] += 1
                ins.then_inc(semaphore, 1)
                eng.wait_ge(semaphore, q * per + n[0])

            def check():
                assert not per or n[0] == per, (n[0], per)
            link.check = check
            return link

        def bc(ap, axis, n):
            v = ap.unsqueeze(axis)
            shape = list(v.shape)
            shape[axis] = n
            return v.broadcast_to(shape)

        def at(buf, q, n=GT):
            if isinstance(q, int):
                return buf[:, q * n:(q + 1) * n]
            return buf[:, bass.ds(q * n, n)]

        def at3(buf, q, lo, hi, n=GT):
            if isinstance(q, int):
                return buf[:, q * n:(q + 1) * n, lo:hi]
            return buf[:, bass.ds(q * n, n), lo:hi]

        def positive(eng, semaphore, value):
            if not isinstance(value, int) or value > 0:
                eng.wait_ge(semaphore, value)

        def rolled(eng, first, last, body, peel):
            for v in range(first, first + peel):
                body(v, v % 2)
            mid = first + peel
            pairs = max(0, (min(last, GROUPS) - mid) // 2)
            assert mid % 2 == 0
            if pairs:
                with eng.Fori(mid // 2, mid // 2 + pairs) as i:
                    body(i * 2, 0)
                    body(i * 2 + 1, 1)
            for v in range(mid + 2 * pairs, last):
                body(v, v % 2)

        def rows1(q):
            if isinstance(q, int):
                return Vrows1[:, q, :, :]
            return Vrows1[:, bass.ds(q, 1), :, :].rearrange("p a c v -> p (a c) v")

        LAG_B, LAG_T, LAG_R = 1, 2, 3
        STEPS = GROUPS + LAG_R

        def has(v, lag):
            return not isinstance(v, int) or 0 <= v - lag < GROUPS

        block_ctx = ExitStack()
        block = block_ctx.enter_context(nc.Block())

        @block.sync
        def _(sp):
            sp.dma_start(cst[:, :], consts[:, :]).then_inc(in_small, 16)
            sp.dma_start(place_f[:, :], places[:, :]).then_inc(in_small, 16)
            sp.dma_start(W0s[:, :], W0[:, :]).then_inc(in_small, 16)
            for c in range(2):
                sp.dma_start(a0s[:, c:c + 1], a0[c * F:(c + 1) * F, :]).then_inc(in_small, 16)
            sp.dma_start(W1e[:, 0:F], W1[:, :]).then_inc(in_small, 16)
            for c in range(2):
                sp.dma_start(a1s[:, 1 - c:2 - c], a1[c * F:(c + 1) * F, :]).then_inc(in_small, 16)
            sp.dma_start(V[0][:, :, 0:F], ent_v).then_inc(in_ent, 16)
            for k in range(GT):
                sp.dma_start(A[:, k, :], adj[k * P:(k + 1) * P, :]).then_inc(adj_in[k], 16)
                if k == 0:
                    sp.dma_start(xs[:, :, :], x_v).then_inc(in_x, 16)
            with sp.Fori(1, GROUPS) as q:
                for k in range(GT):
                    sp.wait_ge(edges_ready, q * GT + (k + 1 - GT))
                    sp.dma_start(A[:, k, :], adj[bass.ds(q * (GT * P) + k * P, P), :]).then_inc(adj_in[k], 16)

            for n, (q0, q1) in enumerate([(0, GROUPS - LAG_R + 1)] + [(q, q + 1) for q in range(GROUPS - LAG_R + 1, GROUPS)]):
                sp.wait_ge(v1_scaled, n + 1)
                sp.dma_start(tab_v[1][:, q0 * GT:q1 * GT, :], V[1][:, q0 * GT:q1 * GT, :]).then_inc(tab_out, 16)

        def gather(L, q, rows):
            for c in range(NCH):
                nc.gpsimd.indirect_dma_start(
                    out=rows[:, c, :], out_offset=None, in_=tab[L][:, :],
                    in_offset=bass.IndirectOffsetOnAxis(ap=idx_all[:, q * NCH + c:q * NCH + c + 1], axis=0),
                ).then_inc(rows_in[L][q % 2], 16)

        @block.gpsimd
        def _(pool):
            nc.gpsimd.memset(ones[:, :], 1.0).then_inc(ready, 1)
            nc.gpsimd.memset(ones2[:, :], 1.0).then_inc(ready, 1)
            nc.gpsimd.memset(V[0][:, :, F + 1:VF], 1.0).then_inc(ready, 1)
            nc.gpsimd.memset(V[1][:, :, F + 1:VF], 1.0).then_inc(ready, 1)

            pool.wait_ge(tab_out, 16)
            for q in range(GROUPS):
                pool.wait_ge(idx_ready, q + 1)
                if q >= 2:
                    pool.wait_ge(nv_done[0], q - 1)
                gather(0, q, Vg[q % 2])
            pool.wait_ge(tab_out, 16 * (1 + LAG_R))
            for q in range(GROUPS):
                if q >= 2:
                    pool.wait_ge(rows_in[1][q % 2], (q // 2) * NCH * 16)
                gather(1, q, rows1(q))

        def pe_scores(pe, L, q):
            pe.wait_ge(wt_ready[L], q + 1)
            for t in range(GT):
                for c in range(CH):
                    last = nc.tensor.transpose(wps[:, t, c * P:(c + 1) * P], wT[:, c * GT + t, :], ident)
            last.then_inc(wps_ready[L], 1)

        def pe_probs(pe, L, q):
            pe.wait_ge(p_ready[L], q + 1)
            for t in range(GT):
                for c in range(CH):
                    last = nc.tensor.transpose(pps[L][:, c, t * P:(t + 1) * P], E1[:, t, c * P:(c + 1) * P], ident)
            last.then_inc(pps_ready[L], 1)

        def pe_values(pe, L, q, rows):
            pe.wait_ge(pt_ready[L], q + 1)
            for t in range(GT):
                for c in range(CH):
                    last = nc.tensor.matmul(nps[:, t, :], PT[:, c * GT + t, :], rows[:, c * GT + t, :],
                                            start=(c == 0), stop=(c == CH - 1))
            last.then_inc(nv_done[L], 1)

        @block.tensor
        def _(pe):
            pe.wait_ge(in_small, 128)
            pe.wait_ge(ready, 4)
            nc.tensor.transpose(sums[0:F, 0:F], W0s[:, :], ident[0:F, 0:F])
            nc.tensor.transpose(sums[0:F, F:2 * F], W1e[:, 0:F], ident[0:F, 0:F]).then_inc(pe_pre, 1)
            pe.wait_ge(dve_pre, 1)
            for c in range(2):
                nc.tensor.matmul(sums[:, 128 + c * F:128 + (c + 1) * F], a0b[:, c, :], W0T[:, :], start=True, stop=True)
            nc.tensor.matmul(sums[0:F, 256:258], W1T[:, :], a1s[:, :], start=True, stop=True).then_inc(pe_pre, 1)
            pe.wait_ge(row_done, 1)
            for t in range(TILES):
                last = nc.tensor.matmul(kbank[:, 0:VF], ones[:, :], V[0][:, t, :],
                                        start=(t == 0), stop=(t == TILES - 1))
            last.then_inc(sum_ready, 1)
            pe.wait_ge(dve_pre, 2)
            pe.wait_ge(sum_copied, 1)

            def tile_codes(q, k):
                pe.wait_ge(edges_ready, q * GT + k + 1)
                positive(pe, codes_copied, q * GT + (k + 1 - 2))
                for b in range(TILES):
                    last = nc.tensor.matmul(low[:, k % 2, b * CODES:(b + 1) * CODES],
                                            edges[:, k % 2, b * P:(b + 1) * P], code_w[:, :], start=True, stop=True)
                last.then_inc(codes_done, 1)

            def offsets(q):
                pe.wait_ge(cnt_ready, q + 1)
                nc.tensor.matmul(offs, before[:, :], cntb[:, :], start=True, stop=True).then_inc(offs_ready, 1)

            def entry_list(q):
                pe.wait_ge(expand_ready, q + 1)
                for c in range(CH):
                    last = nc.tensor.matmul(entp[:, c, :, :], R[:, c * P:(c + 1) * P], Xbd[:, :, :],
                                            start=True, stop=True)
                last.then_inc(entries_ready, 1)

            def key_pieces(q):
                pe.wait_ge(codes_copied, (q + 1) * GT)
                if not isinstance(q, int) or q >= 3:
                    pe.wait_ge(v1_copied, q - 2)
                for n, g0 in enumerate(range(0, CODES, 4)):
                    m = min(4, CODES - g0)
                    positive(pe, keys_copied, q * 3 + n)
                    nc.tensor.matmul(kbank[:, 0:m * P], ones2[:, :], place_w[:, g0 * P:(g0 + m) * P],
                                     start=True, stop=False)
                    for g in range(m):
                        last = nc.tensor.matmul(kbank[:, g * P:(g + 1) * P],
                                                codes[:, g0 + g, :, :].rearrange("p a b -> p (a b)"), ident,
                                                start=False, stop=(g == m - 1))
                    last.then_inc(keyps_ready, 1)

            def hidden_t(q):
                pe.wait_ge(h1_ready, q + 1)
                alone(pe)
                for t in range(GT):
                    last = nc.tensor.transpose(sums[0:F, t * P:(t + 1) * P], h1[:, t, :], ident)
                last.then_inc(h1t_ready, 1)

            def hidden_w(q):
                pe.wait_ge(h1t_copied, q + 1)
                pe.wait_ge(keys_copied, min(3 * (q + 3), 3 * GROUPS) if isinstance(q, int) else 3 * (q + 3))
                for t in range(GT):
                    last = nc.tensor.matmul(whp[:, t, :], h1T[:, t, :], W1e[:, :], start=True, stop=True)
                last.then_inc(wh_ready, 1)

            def step(v, k):
                if has(v, 0):
                    tile_codes(v, 0)
                    tile_codes(v, 1)
                if has(v, LAG_B):
                    offsets(v - LAG_B)
                if has(v, LAG_T):
                    pe_scores(pe, 0, v - LAG_T)
                if has(v, 0):
                    tile_codes(v, 2)
                if has(v, LAG_R):
                    hidden_t(v - LAG_R)
                    hidden_w(v - LAG_R)
                if has(v, LAG_B):
                    entry_list(v - LAG_B)
                if has(v, 0):
                    tile_codes(v, 3)
                    key_pieces(v)
                if has(v, LAG_T):
                    pe_probs(pe, 0, v - LAG_T)
                    pe_values(pe, 0, v - LAG_T, Vg[k])

            rolled(pe, 0, STEPS, step, 4)
            pe.wait_ge(v1_scaled, LAG_R)
            for t in range(TILES):
                last = nc.tensor.matmul(kbank[:, 0:VF], ones[:, :], V[1][:, t, :],
                                        start=(t == 0), stop=(t == TILES - 1))
            last.then_inc(sum_ready, 1)
            pe.wait_ge(over_ready, 1)
            nc.tensor.matmul(sums[0:1, 384:512], over[:, 1:2], ident, start=True, stop=True).then_inc(overT_ready, 1)
            pe.wait_ge(flag_ready, 1)

            def step1(v, k):
                if has(v, 0):
                    positive(pe, exps_done[1], v)
                    pe_scores(pe, 1, v)
                if has(v, 1):
                    pe_probs(pe, 1, v - 1)
                    pe_values(pe, 1, v - 1, rows1(v - 1))

            rolled(pe, 0, GROUPS + 2, step1, 2)

        def act_exps(act, L, q):
            act.wait_ge(bias_ready[L], q + 1)
            for t in range(GT):
                nc.scalar.activation(E1[:, t, :], wps[:, t, :], ACT.Exp, bias=bias1[:, t:t + 1])
                last = nc.scalar.activation(E2[:, t, :], wps[:, t, :], ACT.Exp, bias=bias2[:, t:t + 1], scale=SLOPE)
            last.then_inc(exps_done[L], 1)

        def act_probs(act, L, q):
            act.wait_ge(pps_ready[L], q + 1)
            positive(act, nv_done[L], q)
            for c in range(CH):
                last = nc.scalar.copy(PT[:, c * GT:(c + 1) * GT, :],
                                      pps[L][:, c, :].rearrange("p (t r) -> p t r", t=GT))
            last.then_inc(pt_ready[L], 1)

        def center(src, sums_of, n):
            for t in range(n):
                nc.scalar.activation(y[:, t, :], src[:, t, :], ACT.Square, bias=nmean[:, t:t + 1],
                                     accum_out=sums_of[:, t:t + 1])
                last = nc.scalar.activation(h1[:, t, :], src[:, t, :], ACT.Relu, bias=nmean[:, t:t + 1])
            last.then_inc(h1_ready, 1)

        def act_elu(act, L, q):
            act.wait_ge(neg_ready[L], q + 1)
            nc.scalar.activation(en[:, :, :], neg[:, :, :], ACT.Exp).then_inc(elu_done[L], 1)

        @block.scalar
        def _(act):
            act.wait_ge(sum_ready, 1)
            nc.scalar.copy(sumV[0][:, :], kbank[:, 0:VF]).then_inc(sum_copied, 1)
            act.wait_ge(row_done, 1)
            act.dma_start(tab_v[0], V[0][:, :, :]).then_inc(tab_out, 16)

            def copy_codes(q, k):
                act.wait_ge(codes_done, q * GT + k + 1)
                if k == 0:
                    positive(act, keyps_ready, q * 3)
                nc.scalar.copy(codes[:, :, k, :],
                               low[:, k % 2, 0:TILES * CODES].rearrange("p (b c) -> p c b", c=CODES)
                               ).then_inc(codes_copied, 1)

            def copy_keys(q):
                for n, g0 in enumerate(range(0, CODES, 4)):
                    m = min(4, CODES - g0)
                    act.wait_ge(keyps_ready, q * 3 + (n + 1))
                    if n == 0:
                        positive(act, keys_used, q)
                    nc.scalar.copy(keys[:, g0 * P:(g0 + m) * P], kbank[:, 0:m * P]).then_inc(keys_copied, 1)

            def act_center(q):
                act.wait_ge(mean_ready, q + 1)
                center(at(x1, q), at(ssq, q), GT)

            def copy_hidden(q):
                act.wait_ge(h1t_ready, q + 1)
                nc.scalar.copy(h1T[:, :, :], sums[0:F, :].rearrange("p (t r) -> p t r", t=GT)).then_inc(h1t_copied, 1)

            def copy_values(q):
                act.wait_ge(wh_ready, q + 1)
                nc.scalar.copy(at3(V[1], q, 0, F + 1), whp[:, :, 0:F + 1])
                nc.scalar.copy(at(s[1], q), whp[:, :, F + 1]).then_inc(v1_copied, 1)

            def step(v, k):
                if has(v, 0):
                    copy_codes(v, 0)
                    copy_codes(v, 1)
                if has(v, LAG_R):
                    act_elu(act, 0, v - LAG_R)
                if has(v, 0):
                    copy_codes(v, 2)
                if has(v, LAG_R):
                    act_center(v - LAG_R)
                    copy_hidden(v - LAG_R)
                    copy_values(v - LAG_R)
                if has(v, LAG_T):
                    act_exps(act, 0, v - LAG_T)
                if has(v, 0):
                    copy_codes(v, 3)
                    copy_keys(v)
                if has(v, LAG_T):
                    act_probs(act, 0, v - LAG_T)

            rolled(act, 0, STEPS, step, 4)
            act.wait_ge(sum_ready, 2)
            nc.scalar.copy(sumV[1][:, :], kbank[:, 0:VF]).then_inc(sum_copied, 1)

            def step1(v, k):
                if has(v, 2):
                    act_elu(act, 1, v - 2)
                if has(v, 1):
                    act_probs(act, 1, v - 1)
                if has(v, 0):
                    act_exps(act, 1, v)
                if has(v, 2):
                    q = v - 2
                    act.wait_ge(out_ready, q + 1)
                    dst = out_v[:, q * GT:(q + 1) * GT, :] if isinstance(q, int) else out_v[:, bass.ds(q * GT, GT), :]
                    act.dma_start(dst, outs[k][:, :, :]).then_inc(stored[k], 16)

            rolled(act, 0, GROUPS + 2, step1, 2)
            for k in range(2):
                act.wait_ge(stored[k], 16 * (GROUPS // 2))

        LINKS_SC = 3 + 3 * NEWTON
        LINKS_B1, LINKS_B2, LINKS_B3, LINKS_T2, LINKS_T4A, LINKS_T4B = 10, 3, 11, 5, 4, (3, 1)

        def inverse_root(link, ss, r, v, g):
            link(nc.vector.tensor_scalar(v, ss, 1.0 / F, EPS, ALU.mult, ALU.add))
            ri = r.bitcast(i32)
            link(nc.vector.tensor_scalar(ri, v.bitcast(i32), 1, None, ALU.logical_shift_right))
            link(nc.vector.tensor_scalar(ri, ri, -1.0, float(0x5F3759DF), ALU.mult, ALU.add))
            for _ in range(NEWTON):
                link(nc.vector.tensor_tensor(g, r, r, ALU.mult))
                link(nc.vector.scalar_tensor_tensor(g, g, -0.5, v, ALU.mult, ALU.mult))
                link(nc.vector.scalar_tensor_tensor(r, g, 1.5, r, ALU.add, ALU.mult))

        def scale_values(link, V1t, s1t, ss, n):
            r, v, g = (rstd[:, i, 0:n] for i in range(3))
            inverse_root(link, ss, r, v, g)
            nc.vector.tensor_tensor(s1t, s1t, r, ALU.mult)
            return nc.vector.tensor_tensor(V1t, V1t, bc(r, 2, F + 1), ALU.mult)

        def biases(link, L, q, k, sAP, n):
            link(nc.vector.tensor_scalar(Mc[:, 0:n], Mx[:, 0:n], FLOOR, None, ALU.max))
            nc.vector.tensor_scalar(empty[:, k, 0:n], Mx[:, 0:n], FLOOR, None, ALU.is_lt)
            link(nc.vector.tensor_tensor(sM[:, 0:n], Mc[:, 0:n], sAP, ALU.add))
            link(nc.vector.scalar_tensor_tensor(guard[:, 0:n], sM[:, 0:n], SLOPE, sM[:, 0:n], ALU.mult, ALU.max))
            link(nc.vector.tensor_tensor(bias1[:, 0:n], sAP, guard[:, 0:n], ALU.subtract))
            return nc.vector.scalar_tensor_tensor(bias2[:, 0:n], sAP, SLOPE, guard[:, 0:n], ALU.mult, ALU.subtract)

        def dve_masked(dve, L, q, k, rows):
            dve.wait_ge(rows_in[L][k], (q - k + 2) * (NCH * 8))
            pq = pen[:, q, :, 0:P] if isinstance(q, int) else pen[:, bass.ds(q, 1), :, 0:P].rearrange("p a b c -> p (a b) c")
            nc.vector.tensor_tensor(wT[:, :, :], pq, rows[:, :, F:F + 1].broadcast_to([P, NCH, P]),
                                    ALU.add).then_inc(wt_ready[L], 1)

        def dve_guards(dve, L, q, k):
            link = linker(dve, link_t2[L], q, LINKS_T2)
            dve.wait_ge(wps_ready[L], q + 1)
            link(nc.vector.reduce_max(Mx[:, :], wps, X))
            biases(link, L, q, k, at(s[L], q), GT).then_inc(bias_ready[L], 1)
            link.check()

        def dve_weights(dve, L, q):
            dve.wait_ge(exps_done[L], q + 1)
            nc.vector.tensor_tensor(E1[:, :, :], E1[:, :, :], E2[:, :, :], ALU.max).then_inc(p_ready[L], 1)

        def attended(link, L, q, k, n, npsAP, tiles):
            link(nc.vector.tensor_tensor(att[:, 0:n, :], bc(sumV[L][:, :], 1, n),
                                         bc(empty[:, k, 0:n], 2, VF), ALU.mult))
            link(nc.vector.tensor_tensor(att[:, 0:n, :], att[:, 0:n, :], npsAP, ALU.add))
            link(nc.vector.reciprocal(rden[:, 0:n], att[:, 0:n, F + 1]))
            last = nc.vector.tensor_tensor(hp[:, 0:n, :], att[:, 0:n, 0:F], bc(rden[:, 0:n], 2, F), ALU.mult)
            link(last)
            if L == 0:
                link(nc.vector.tensor_tensor(hp[:, 0:n, :], hp[:, 0:n, :], tiles(h0), ALU.add))
            return nc.vector.tensor_scalar(neg[:, 0:n, :], hp[:, 0:n, :], 0.0, None, ALU.min)

        def dve_attended(dve, L, q, k):
            link = linker(dve, link_t4a[L], q, LINKS_T4A + (L == 0))
            dve.wait_ge(nv_done[L], q + 1)
            attended(link, L, q, k, GT, nps, lambda b: at(b, q)).then_inc(neg_ready[L], 1)
            link.check()

        def dve_rows(dve, L, q, k):
            link = linker(dve, link_t4b[L], q, LINKS_T4B[L])
            dve.wait_ge(elu_done[L], q + 1)
            link(nc.vector.scalar_tensor_tensor(y[:, :, :], hp[:, :, :], 0.0, at(xs if L == 0 else x1, q),
                                                ALU.max, ALU.add))
            if L == 0:
                xq = at(x1, q)
                link(nc.vector.scalar_tensor_tensor(xq, en[:, :, :], -1.0, y[:, :, :], ALU.add, ALU.add))
                alone(dve)
                link(nc.vector.reduce_sum(mean[:, :], xq, X))
                nc.vector.tensor_scalar(nmean[:, :], mean[:, :], -1.0 / F, None, ALU.mult).then_inc(mean_ready, 1)
            else:
                if not isinstance(q, int) or q >= 2:
                    dve.wait_ge(stored[k], (q - k) * 8)
                nc.vector.scalar_tensor_tensor(outs[k][:, :, :], en[:, :, :], -1.0, y[:, :, :],
                                               ALU.add, ALU.add).then_inc(out_ready, 1)
            link.check()

        @block.vector
        def _(dve):
            link = linker(dve, link_pre)
            nc.vector.memset(over[:, :], 0.0)
            dve.wait_ge(in_small, 128)
            nc.vector.tensor_copy(code_w[:, :], cst[:, where["code"][0]:where["code"][1]])
            nc.vector.tensor_copy(before[:, :], cst[:, where["before"][0]:where["before"][1]])
            nc.vector.tensor_copy(bit_w[:, :], cst[:, where["bit"][0]:where["bit"][1]])
            nc.vector.tensor_copy(kept[:, TOP + 1:TOP + 2], cst[:, where["block"][0]:where["block"][1]])
            nc.vector.tensor_copy(place_w[:, :], place_f[:, :])
            nc.vector.tensor_copy(a0b[:, :, :], a0s[:, :].unsqueeze(2).broadcast_to([F, 2, P]))
            dve.wait_ge(pe_pre, 1)
            nc.vector.tensor_copy(W0T[:, :], sums[0:F, 0:F])
            nc.vector.tensor_copy(W1T[:, :], sums[0:F, F:2 * F]).then_inc(dve_pre, 1)
            dve.wait_ge(pe_pre, 2)
            nc.vector.tensor_copy(W1e[:, F:F + 2], sums[0:F, 256:258])
            nc.vector.tensor_copy(wbc[:, :, :], sums[:, 128:256].rearrange("p (c f) -> p c f", c=2)
                                  ).then_inc(dve_pre, 1)
            dve.wait_ge(dve_pre, 2)
            dve.wait_ge(in_ent, 16)
            link(nc.vector.tensor_tensor(lnc0, V[0][:, :, 0:F], bc(wbc[:, 1, :], 1, TILES), ALU.mult))
            nc.vector.reduce_sum(V[0][:, :, F], lnc0, X).then_inc(row_done, 1)
            dve.wait_ge(in_x, 16)
            r, v, g = (rstd[:, i, :] for i in range(3))
            link(nc.vector.reduce_sum(v, xs[:, :, :], X))
            link(nc.vector.tensor_scalar(g, v, -1.0 / F, None, ALU.mult))
            link(nc.vector.tensor_tensor(lnc0, xs[:, :, :], bc(g, 2, F), ALU.add))
            link(nc.vector.tensor_tensor(lnq0, lnc0, lnc0, ALU.mult))
            link(nc.vector.reduce_sum(ssq[:, :], lnq0, X))
            inverse_root(link, ssq[:, :], r, v, g)
            link(nc.vector.tensor_scalar(lnc0, lnc0, 0.0, None, ALU.max))
            link(nc.vector.tensor_tensor(h0[:, :, :], lnc0, bc(r, 2, F), ALU.mult))
            link(nc.vector.tensor_tensor(lnc0, h0[:, :, :], bc(wbc[:, 0, :], 1, TILES), ALU.mult))
            link(nc.vector.reduce_sum(s[0][:, :], lnc0, X))

            def tile_edges(q, k):
                dve.wait_ge(adj_in[k], (q + 1) * 16)
                positive(dve, codes_done, q * GT + (k + 1 - 2))
                nc.vector.tensor_scalar(edges[:, k % 2, :], A[:, k, :], 0.0, None, ALU.is_gt).then_inc(edges_ready, 1)

            def best_keys(q):
                link = linker(dve, link_b1, q, LINKS_B1)
                dve.wait_ge(keys_copied, q * 3 + 3)
                alone(dve)
                for n in range(NSEG):
                    last = nc.vector.max(slots[:, n, :], keys[:, n * SEG:(n + 1) * SEG])
                last.then_inc(keys_used, 1)
                dve.wait_ge(keys_used, q + 1)
                link(nc.vector.reduce_max(over[:, 1:2], slots[:, :, 7], X))
                flat = slots[:, :, :].rearrange("p a b -> p (a b)")
                for r in range(TOP // 8):
                    alone(dve)
                    link(nc.vector.max(top[:, 8 * r:8 * r + 8], flat))
                    if r < TOP // 8 - 1:
                        alone(dve)
                        link(nc.vector.match_replace(flat, top[:, 8 * r:8 * r + 8], flat, 0.0))
                nc.vector.tensor_tensor(over[:, 2:3], over[:, 1:2], top[:, TOP - 1:TOP], ALU.max)
                link(nc.vector.tensor_scalar(isv[:, :], top[:, :], VALID, None, ALU.is_ge))
                link(nc.vector.reduce_sum(cnt[:, :], isv[:, :], X))
                link(nc.vector.tensor_tensor(over[:, 0:1], over[:, 0:1], over[:, 2:3], ALU.max))
                link(nc.vector.tensor_tensor(kept[:, 0:TOP], top[:, :], isv[:, :], ALU.mult))
                nc.vector.tensor_copy(cntb[:, :], cnt[:, :]).then_inc(cnt_ready, 1)
                link.check()

            def expand(q):
                link = linker(dve, link_b2, q, LINKS_B2)
                dve.wait_ge(offs_ready, q + 1)
                nc.vector.tensor_copy(kept[:, TOP:TOP + 1], offs)
                link(nc.vector.tensor_tensor(end[:, :], cnt[:, :], offs, ALU.add))
                nc.vector.tensor_scalar(R0[:, :], slot_no, kept[:, TOP:TOP + 1], None, ALU.is_ge)
                link(nc.vector.tensor_scalar(over[:, 3:4], end[:, :], float(ENTRIES), 2.0 * VALID, ALU.is_gt, ALU.mult))
                link(nc.vector.tensor_tensor(over[:, 0:1], over[:, 0:1], over[:, 3:4], ALU.max))
                nc.vector.tensor_tensor(Xbd[:, :, :], bc(kept[:, :], 1, GT), bc(tile_of, 2, TOP + 2), ALU.mult)
                nc.vector.scalar_tensor_tensor(R[:, :], slot_no, end[:, 0:1], R0[:, :],
                                               ALU.is_lt, ALU.mult).then_inc(expand_ready, 1)
                link.check()

            def decode(q):
                link = linker(dve, link_b3, q, LINKS_B3)
                dve.wait_ge(entries_ready, q + 1)
                d3 = dist[:, :].rearrange("p (c g) -> p c g", c=CH)
                link(nc.vector.tensor_tensor(d3, bc(entry_no, 2, GT), entp[:, :, :, TOP], ALU.subtract))
                link(nc.vector.tensor_tensor(hit[:, :, :], bc(top_no, 1, NCH), bc(dist[:, :], 2, TOP), ALU.is_equal))
                e3 = entp.rearrange("p c g k -> p (c g) k")
                link(nc.vector.tensor_tensor(hit[:, :, :], hit[:, :, :], e3[:, :, 0:TOP], ALU.mult))
                link(nc.vector.reduce_sum(dist[:, :], hit[:, :, :], X))
                link(nc.vector.tensor_copy(keyi[:, :], dist[:, :]))
                nc.vector.tensor_scalar(grp[:, :], keyi[:, :], 7, 15, ALU.logical_shift_right, ALU.bitwise_and)
                nc.vector.tensor_scalar(col[:, :], keyi[:, :], 127, None, ALU.bitwise_and)
                link(nc.vector.tensor_scalar(code[:, :], keyi[:, :], POSBITS, None, ALU.logical_shift_right))
                link(nc.vector.tensor_tensor(biti[:, :, :], bc(code[:, :], 2, ROWS), bc(bit_w[:, :], 1, NCH),
                                             ALU.bitwise_and))
                nc.vector.scalar_tensor_tensor(at(idx_all, q, NCH), e3[:, :, TOP + 1], float(P), col[:, :],
                                               ALU.mult, ALU.add).then_inc(idx_ready, 1)
                link(nc.vector.tensor_scalar(bitb[:, :, :], biti[:, :, :], 0.0, None, ALU.is_gt))
                link(nc.vector.tensor_tensor(grpb[:, :, :], bc(group_no, 1, NCH), bc(grp[:, :], 2, CODES),
                                             ALU.is_equal))
                m4 = mask[:, :, :].rearrange("p n (c r) -> p n c r", c=CODES)
                link(nc.vector.tensor_tensor(m4, bc(grpb[:, :, :], 3, ROWS), bc(bitb[:, :, :], 2, CODES), ALU.mult))
                pq = pen[:, q, :, :] if isinstance(q, int) else pen[:, bass.ds(q, 1), :, :].rearrange("p a b c -> p (a b) c")
                link(nc.vector.tensor_scalar(pq, mask[:, :, :], BIG, -BIG, ALU.mult, ALU.add))
                link.check()

            def step(v, k):
                if has(v, 0):
                    tile_edges(v, 0)
                    tile_edges(v, 1)
                if has(v, LAG_B):
                    best_keys(v - LAG_B)
                if has(v, LAG_R):
                    dve_attended(dve, 0, v - LAG_R, 1 - k)
                if has(v, LAG_T):
                    dve_masked(dve, 0, v - LAG_T, k, Vg[k])
                if has(v, 0):
                    tile_edges(v, 2)
                if has(v, LAG_R):
                    dve_rows(dve, 0, v - LAG_R, 1 - k)
                if has(v, LAG_B):
                    expand(v - LAG_B)
                if has(v, LAG_T):
                    dve_guards(dve, 0, v - LAG_T, k)
                if has(v, 0):
                    tile_edges(v, 3)
                if has(v, LAG_B):
                    decode(v - LAG_B)
                if has(v, LAG_T):
                    dve_weights(dve, 0, v - LAG_T)

                if isinstance(v, int) and v >= GROUPS:
                    scaled(0 if v == GROUPS else v - LAG_R, v - LAG_R + 1)

            def scaled(q0, q1):
                link = linker(dve, link_sc, len(scale_links), LINKS_SC)
                scale_links.append(q1)
                dve.wait_ge(v1_copied, q1)
                t0, t1 = q0 * GT, q1 * GT
                scale_values(link, V[1][:, t0:t1, 0:F + 1], s[1][:, t0:t1], ssq[:, t0:t1], t1 - t0
                             ).then_inc(v1_scaled, 1)
                link.check()

            scale_links = []
            rolled(dve, 0, STEPS, step, 4)
            nc.vector.tensor_copy(over[:, 1:2], over[:, 0:1]).then_inc(over_ready, 1)
            link = linker(dve, link_end)
            dve.wait_ge(overT_ready, 1)
            link(nc.vector.reduce_max(end[0:1, :], sums[0:1, 384:512], X))
            nc.vector.tensor_scalar(flag[:, :], end[0:1, :], VALID, None, ALU.is_ge).then_inc(flag_ready, 1)
            dve.wait_ge(sum_copied, 2)

            def step1(v, k):
                if has(v, 2):
                    dve_attended(dve, 1, v - 2, k)
                if has(v, 0):
                    dve_masked(dve, 1, v, k, rows1(v))
                if has(v, 2):
                    dve_rows(dve, 1, v - 2, k)
                if has(v, 1):
                    dve_weights(dve, 1, v - 1)
                if has(v, 0):
                    dve_guards(dve, 1, v, k)

            rolled(dve, 0, GROUPS + 2, step1, 2)

        block_ctx.close()
        block_ctx = ExitStack()
        block = block_ctx.enter_context(nc.Block())
        score = A[:, 1, :].bitcast(fp32)
        ex1 = A[:, 2, :].bitcast(fp32)
        ex2 = A[:, 3, :].bitcast(fp32)
        trow = edges[:, :, :].rearrange("p a b -> p (a b)").bitcast(fp32)
        diag = wT[:, 0, :]
        UNITS = TILES // 4
        g = {n: sem("g_" + n) for n in (
            "x_in", "adj_in", "score_ready", "diag_ready", "spread", "spread_copied", "sum_ready", "sum_copied",
            "bias_ready", "exps_done", "p_ready", "turned", "turned_copied", "values_done", "neg_ready",
            "elu_done", "mean_ready", "v1_scaled", "h1t_ready", "h1t_copied", "wh_ready", "v1_copied", "out_ready", "stored")}
        g_link = {n: sem("g_link_" + n) for n in ("a0", "a1", "b0", "b1", "c0", "c1", "sc")}

        def one(buf, t):
            return buf[:, t:t + 1] if isinstance(t, int) else buf[:, bass.ds(t, 1)]

        def one3(buf, t, lo, hi):
            return buf[:, t:t + 1, lo:hi] if isinstance(t, int) else buf[:, bass.ds(t, 1), lo:hi]

        def each_tile(eng, body, peel=0):
            for t in range(peel):
                body(t)
            with eng.Fori(peel, TILES) as t:
                body(t)

        def general(eng, program):
            with eng.If(eng.value_load(flag[0:1, 0:1], min_val=0, max_val=1) > 0):
                program()

        @block.sync
        def _(sp):
            def program():
                sp.dma_start(xs[:, :, :], x_v).then_inc(g["x_in"], 16)
                for L in range(2):
                    def tile(t):
                        if L or not isinstance(t, int):
                            sp.wait_ge(g["score_ready"], L * TILES + t)
                        sp.dma_start(A[:, 0, :], adj[bass.ds(t * P, P), :]).then_inc(g["adj_in"], 16)
                    each_tile(sp, tile, 1)
            general(sp, program)

        @block.tensor
        def _(pe):
            def program():
                for L in range(2):
                    if L:
                        pe.wait_ge(g["v1_scaled"], 1)
                        for t in range(TILES):
                            last = nc.tensor.matmul(kbank[:, 0:VF], ones[:, :], V[1][:, t, :],
                                                    start=(t == 0), stop=(t == TILES - 1))
                        last.then_inc(g["sum_ready"], 1)
                        pe.wait_ge(g["sum_copied"], 1)

                    def spread(t):
                        pe.wait_ge(g["diag_ready"], L * TILES + t + 1)
                        nc.tensor.matmul(kbank[:, 0:P], ones[:, :], diag, start=True, stop=True).then_inc(g["spread"], 1)
                    each_tile(pe, spread)

                    def turn(t, u):
                        if u == 0:
                            pe.wait_ge(g["p_ready"], L * TILES + t + 1)
                        if L or u or not isinstance(t, int):
                            if not (L == 0 and isinstance(t, int) and u < 2):
                                pe.wait_ge(g["turned_copied"], (L * TILES + t) * UNITS + (u - 1))
                        for b in range(4):
                            last = nc.tensor.transpose(work[:, u % 2, b * P:(b + 1) * P],
                                                       ex1[:, (4 * u + b) * P:(4 * u + b + 1) * P], ident)
                        last.then_inc(g["turned"], 1)

                    def values(t, u):
                        pe.wait_ge(g["turned_copied"], (L * TILES + t) * UNITS + (u + 1))
                        for b in range(4):
                            last = nc.tensor.matmul(nps[:, 0, :], PT[:, 4 * (u % 2) + b, :], V[L][:, 4 * u + b, :],
                                                    start=(u + b == 0), stop=(4 * u + b == TILES - 1))
                        last.then_inc(g["values_done"], 1)

                    def tile(t):
                        turn(t, 0)
                        for u in range(UNITS):
                            if u + 1 < UNITS:
                                turn(t, u + 1)
                            values(t, u)
                        if L == 0:
                            pe.wait_ge(h1_ready, GROUPS + t + 1)
                            alone(pe)
                            nc.tensor.transpose(sums[0:F, P:2 * P], h1[:, 0, :], ident).then_inc(g["h1t_ready"], 1)
                            pe.wait_ge(g["h1t_copied"], t + 1)
                            nc.tensor.matmul(whp[:, 0, :], h1T[:, 0, :], W1e[:, :], start=True, stop=True
                                             ).then_inc(g["wh_ready"], 1)
                    each_tile(pe, tile, 1)
            general(pe, program)

        @block.scalar
        def _(act):
            def program():
                for L in range(2):
                    if L:
                        act.wait_ge(g["sum_ready"], 1)
                        nc.scalar.copy(sumV[1][:, :], kbank[:, 0:VF]).then_inc(g["sum_copied"], 1)

                    def spread(t):
                        act.wait_ge(g["spread"], L * TILES + t + 1)
                        nc.scalar.copy(trow[:, t * P:(t + 1) * P] if isinstance(t, int) else trow[:, bass.ds(t * P, P)],
                                       kbank[:, 0:P]).then_inc(g["spread_copied"], 1)
                    each_tile(act, spread)

                    def tile(t):
                        act.wait_ge(g["bias_ready"], L * TILES + t + 1)
                        nc.scalar.activation(ex1, score, ACT.Exp, bias=bias1[:, 0:1])
                        nc.scalar.activation(ex2, score, ACT.Exp, bias=bias2[:, 0:1], scale=SLOPE
                                             ).then_inc(g["exps_done"], 1)
                        for u in range(UNITS):
                            act.wait_ge(g["turned"], (L * TILES + t) * UNITS + (u + 1))
                            if not (L == 0 and isinstance(t, int) and u < 2):
                                act.wait_ge(g["values_done"], (L * TILES + t) * UNITS + (u - 1))
                            nc.scalar.copy(PT[:, 4 * (u % 2):4 * (u % 2) + 4, :],
                                           work[:, u % 2, :].rearrange("p (b r) -> p b r", b=4)
                                           ).then_inc(g["turned_copied"], 1)
                        act.wait_ge(g["neg_ready"], L * TILES + t + 1)
                        nc.scalar.activation(en[:, 0, :], neg[:, 0, :], ACT.Exp).then_inc(g["elu_done"], 1)
                        if L == 0:
                            act.wait_ge(g["mean_ready"], t + 1)
                            center(one3(x1, t, 0, F), one(ssq, t), 1)
                            act.wait_ge(g["h1t_ready"], t + 1)
                            nc.scalar.copy(h1T[:, 0, :], sums[0:F, P:2 * P]).then_inc(g["h1t_copied"], 1)
                            act.wait_ge(g["wh_ready"], t + 1)
                            nc.scalar.copy(one3(V[1], t, 0, F + 1), whp[:, 0:1, 0:F + 1])
                            nc.scalar.copy(one(s[1], t), whp[:, 0, F + 1:F + 2]).then_inc(g["v1_copied"], 1)
                        else:
                            act.wait_ge(g["out_ready"], t + 1)
                            act.dma_start(out[bass.ds(t * P, P), :], outs[0][:, 0, :]).then_inc(g["stored"], 16)
                    each_tile(act, tile, 1)
                act.wait_ge(g["stored"], 16 * TILES)
            general(act, program)

        @block.vector
        def _(dve):
            def program():
                dve.wait_ge(g["x_in"], 16)
                for L in range(2):
                    if L:
                        dve.wait_ge(g["v1_copied"], TILES)
                        scale_values(linker(dve, g_link["sc"]), V[1][:, :, 0:F + 1], s[1][:, :], ssq[:, :], TILES
                                     ).then_inc(g["v1_scaled"], 1)
                        dve.wait_ge(g["v1_scaled"], 1)

                    def spread(t):
                        if L or not isinstance(t, int):
                            dve.wait_ge(g["spread_copied"], L * TILES + t)
                        nc.vector.tensor_scalar(diag, ident, one3(V[L], t, F, F + 1).rearrange("p a b -> p (a b)"),
                                                None, ALU.mult).then_inc(g["diag_ready"], 1)
                    each_tile(dve, spread, 1)
                    dve.wait_ge(g["spread_copied"], (L + 1) * TILES)

                    def tile(t):
                        link = linker(dve, g_link[f"a{L}"], t, 7)
                        dve.wait_ge(g["adj_in"], (L * TILES + t + 1) * 16)
                        nc.vector.tensor_scalar(score, A[:, 0, :], 0.0, -BIG, ALU.is_le, ALU.mult
                                                ).then_inc(g["score_ready"], 1)
                        dve.wait_ge(g["score_ready"], L * TILES + t + 1)
                        link(nc.vector.tensor_tensor(score, score, trow, ALU.add))
                        link(nc.vector.reduce_max(Mx[:, 0:1], score, X))
                        link(nc.vector.tensor_copy(sT, one(s[L], t)))
                        biases(link, L, t, 0, sT, 1).then_inc(g["bias_ready"], 1)
                        link.check()
                        dve.wait_ge(g["exps_done"], L * TILES + t + 1)
                        nc.vector.tensor_tensor(ex1, ex1, ex2, ALU.max).then_inc(g["p_ready"], 1)
                        link = linker(dve, g_link[f"b{L}"], t, LINKS_T4A + (L == 0))
                        dve.wait_ge(g["values_done"], (L * TILES + t + 1) * UNITS)
                        attended(link, L, t, 0, 1, nps[:, 0:1, :], lambda b: one3(b, t, 0, F)).then_inc(g["neg_ready"], 1)
                        link.check()
                        link = linker(dve, g_link[f"c{L}"], t, LINKS_T4B[L])
                        dve.wait_ge(g["elu_done"], L * TILES + t + 1)
                        link(nc.vector.scalar_tensor_tensor(y[:, 0:1, :], hp[:, 0:1, :], 0.0, one3(xs, t, 0, F),
                                                            ALU.max, ALU.add))
                        if L == 0:
                            link(nc.vector.scalar_tensor_tensor(one3(xs, t, 0, F), en[:, 0:1, :], -1.0, y[:, 0:1, :],
                                                                ALU.add, ALU.add))
                            alone(dve)
                            link(nc.vector.reduce_sum(mean[:, 0:1], one3(xs, t, 0, F), X))
                            nc.vector.tensor_scalar(nmean[:, 0:1], mean[:, 0:1], -1.0 / F, None, ALU.mult
                                                    ).then_inc(g["mean_ready"], 1)
                        else:
                            if not isinstance(t, int):
                                dve.wait_ge(g["stored"], t * 16)
                            nc.vector.scalar_tensor_tensor(outs[0][:, 0:1, :], en[:, 0:1, :], -1.0, y[:, 0:1, :],
                                                           ALU.add, ALU.add).then_inc(g["out_ready"], 1)
                        link.check()
                    each_tile(dve, tile, 1)
            general(dve, program)
        block_ctx.close()


_INS = ['x', 'adj', 'L0_gnn_entity_embs', 'L0_gnn_W', 'L0_gnn_a', 'L1_gnn_W', 'L1_gnn_a']
_OUTS = [((4096, 64), 'float32')]


def shape_constants():
    import numpy as np

    where, width = const_columns()
    c = np.zeros((P, width), np.float32)
    p = np.arange(P)

    def put(name, v):
        c[:, where[name][0]:where[name][1]] = v

    put("ident", np.eye(P))
    off = p[:, None] - ROWS * np.arange(CODES)[None, :]
    put("code", np.where((off >= 0) & (off < ROWS), VALID * 2.0 ** np.clip(off, 0, ROWS), 0.0))
    put("before", (p[:, None] < p[None, :]) & (p[:, None] // TILES == p[None, :] // TILES))
    put("tile", p[:, None] // TILES == np.arange(GT)[None, :])
    put("block", (p % TILES)[:, None])
    put("slot", np.arange(ENTRIES)[None, :])
    put("entry", p[:, None] + P * np.arange(CH)[None, :])
    put("top", np.arange(TOP)[None, :])
    put("group", np.arange(CODES)[None, :])
    put("bit", 2.0 ** np.arange(ROWS)[None, :])
    pos = np.arange(POS)
    return c, np.stack([pos // P * P, pos % P]).astype(np.float32)


def kernel(**inputs):
    import numpy as _np
    import concourse.bacc as _bacc
    from concourse import mybir as _mybir
    from concourse.bass_utils import run_bass_kernel_spmd as _run

    nc = _bacc.Bacc("TRN2", target_bir_lowering=False, num_devices=1)
    arrays, args = {}, []

    def add(name, a):
        arrays[name] = a
        args.append(nc.dram_tensor(name, a.shape, _mybir.dt.from_np(a.dtype), kind="ExternalInput").ap())

    for name in _INS:
        add(f"in_{name}_dram", _np.ascontiguousarray(inputs[name]))
    consts, places = shape_constants()
    add("const_tables_dram", consts)
    add("const_places_dram", places)
    for n in range(2):
        args.append(nc.dram_tensor(f"value_table{n}", (N, VF), _mybir.dt.float32, kind="Internal").ap())
    for i, (shape, dtype) in enumerate(_OUTS):
        dt = _mybir.dt.from_np(_np.dtype(dtype))
        args.append(nc.dram_tensor(f"out_{i}_dram", shape, dt, kind="ExternalOutput").ap())
    graph_attention(nc, *args)
    r = _run(nc, [arrays], core_ids=[0])
    return r.results[0]["out_0_dram"]
```
